# Optimizing a Trainium2 kernel written in Bass

```python
import numpy as np
import jax
import jax.numpy as jnp

def _softmax(x, axis=-1):
    return jax.nn.softmax(x, axis=axis)

def _gelu(x):
    return jax.nn.gelu(x, approximate=True)

def _silu(x):
    return jax.nn.silu(x)

def _sigmoid(x):
    return jax.nn.sigmoid(x)

def _layernorm(x, axis=-1, eps=1e-05):
    m = jnp.mean(x, axis=axis, keepdims=True)
    v = jnp.var(x, axis=axis, keepdims=True)
    return (x - m) / jnp.sqrt(v + eps)

def _scatter_add(tgt, idx, src, axis=0):
    return tgt.at[idx].add(src)

def _segment_sum(src, seg, n):
    return jax.ops.segment_sum(src, seg, n)
kernel_name = 'mk_decoder_preln_d2_seqx_r4_fccd82'

def setup_inputs(seed: int=0):
    np.random.seed(seed)
    _w = jnp.asarray

    def _rec_inputs():
        import jax
        import jax.numpy as jnp
        _rk = jax.random.key(seed)
        x = -0.0005146 + 1 * jax.random.normal(jax.random.fold_in(_rk, 1), (8, 256, 256), jnp.float32)
        _lenS = 256 - jax.random.randint(jax.random.fold_in(_rk, 7), (8,), 0, max(1, 256 // 4) + 1, jnp.int32)
        _lenS2 = 256 - jax.random.randint(jax.random.fold_in(_rk, 8), (8,), 0, max(1, 256 // 4) + 1, jnp.int32)
        _ctx_1024P = jax.random.normal(jax.random.fold_in(_rk, 11), (8, 16, 256), jnp.float32)
        _ctx_1024c = jax.random.dirichlet(jax.random.fold_in(_rk, 511), 0.3 * jnp.ones((16,), jnp.float32), (8, 256))
        _ctx_1024t = jnp.einsum('bsk,bkd->bsd', _ctx_1024c, _ctx_1024P)
        _ctx_1024t = _ctx_1024t * jax.lax.rsqrt(jnp.mean(jnp.square(_ctx_1024t)) + 1e-12) * 0.953939
        ctx_1024 = 7.22013e-05 + 1.00017 * (_ctx_1024t + 0.3 * jax.random.normal(jax.random.fold_in(_rk, 611), (8, 256, 256), jnp.float32))
        fside_BxSxS2_0 = jax.random.uniform(jax.random.fold_in(_rk, 13), (8, 256, 256), jnp.float32, 0.0, 1)
        _validS = jnp.arange(256)[None, :] < _lenS[:, None]
        _validS2 = jnp.arange(256)[None, :] < _lenS2[:, None]
        _causal = jnp.tril(jnp.ones((256, 256), dtype=bool))
        mask_Bx1xSxS2_if1 = jnp.where(jnp.ones((8, 1, 256, 256), dtype=bool), 1, 0).astype(jnp.int32)
        return (x, ctx_1024, fside_BxSxS2_0, mask_Bx1xSxS2_if1)
    x, ctx_1024, fside_BxSxS2_0, mask_Bx1xSxS2_if1 = _rec_inputs()

    def _L0_attn_setup():
        import jax, jax.numpy as jnp
        import numpy as np
        D = 256
        H = 16
        DH = D // H
        key = jax.random.key(seed)
        k1, k2, k3 = jax.random.split(key, 3)
        x = jax.random.normal(k1, (2, 512, D), dtype=jnp.float32)
        w_qkv = jax.random.normal(k2, (3 * D, D), dtype=jnp.float32) * D ** (-0.5)
        w_proj = jax.random.normal(k3, (D, D), dtype=jnp.float32) * D ** (-0.5)
        return {'x': x, 'w_qkv': w_qkv, 'w_proj': w_proj}
    _L0_attn_all = _L0_attn_setup()
    _L0_attn_in = {k: v for k, v in _L0_attn_all.items() if k in ('w_qkv', 'w_proj')}
    del _L0_attn_all

    def _L0_xattn_setup():
        import jax, jax.numpy as jnp
        import numpy as np
        DIM = 256
        HEADS = 16
        DS = 4
        key = jax.random.key(seed)
        ks = jax.random.split(key, 10)
        B, N, M = (2, 256, 1024)
        s = 0.02
        return {'x': jax.random.normal(ks[0], (B, M, DIM), jnp.float32), 'l': jax.random.normal(ks[1], (B, N, DIM), jnp.float32), 'Wq': jax.random.normal(ks[2], (DIM, DIM), jnp.float32) * s, 'bq': jnp.zeros((DIM,), jnp.float32), 'Wk': jax.random.normal(ks[3], (DIM, DIM), jnp.float32) * s, 'bk': jnp.zeros((DIM,), jnp.float32), 'Wv': jax.random.normal(ks[4], (DIM, DIM), jnp.float32) * s, 'bv': jnp.zeros((DIM,), jnp.float32), 'Wo': jax.random.normal(ks[5], (DIM, DIM), jnp.float32) * s, 'bo': jnp.zeros((DIM,), jnp.float32)}
    _L0_xattn_all = _L0_xattn_setup()
    _L0_xattn_in = {k: v for k, v in _L0_xattn_all.items() if k in ('Wq', 'bq', 'Wk', 'bk', 'Wv', 'bv', 'Wo', 'bo')}
    del _L0_xattn_all

    def _L0_ffn_setup():
        import jax, jax.numpy as jnp
        import numpy as np
        B, S, D_MODEL, D_HIDDEN = (4, 512, 256, 1024)

        def act_quant(x):
            scale = 127.0 / jnp.clip(jnp.max(jnp.abs(x), axis=-1, keepdims=True), 1e-05)
            return jnp.clip(jnp.round(x * scale), -128, 127) / scale

        def weight_quant(w):
            scale = 1.0 / jnp.clip(jnp.mean(jnp.abs(w)), 1e-05)
            return jnp.clip(jnp.round(w * scale), -1, 1) / scale

        def bit_linear(x, w):
            xq = x + jax.lax.stop_gradient(act_quant(x) - x)
            wq = w + jax.lax.stop_gradient(weight_quant(w) - w)
            return jnp.einsum('bsd,hd->bsh', xq, wq)

        def depthwise_conv1d(x_bcl, w, b):
            y = jax.lax.conv_general_dilated(x_bcl, w, window_strides=(1,), padding=[(1, 1)], dimension_numbers=('NCH', 'OIH', 'NCH'), feature_group_count=x_bcl.shape[1])
            return y + b[None, :, None]
        key = jax.random.key(seed)
        ks = jax.random.split(key, 5)
        lim1 = 1.0 / np.sqrt(D_MODEL)
        lim2 = 1.0 / np.sqrt(D_HIDDEN)
        limc = 1.0 / np.sqrt(3.0)
        return {'x': jax.random.normal(ks[0], (B, S, D_MODEL), dtype=jnp.float32), 'w1': jax.random.uniform(ks[1], (D_HIDDEN, D_MODEL), jnp.float32, -lim1, lim1), 'conv_w': jax.random.uniform(ks[2], (D_HIDDEN, 1, 3), jnp.float32, -limc, limc), 'conv_b': jax.random.uniform(ks[3], (D_HIDDEN,), jnp.float32, -limc, limc), 'w2': jax.random.uniform(ks[4], (D_MODEL, D_HIDDEN), jnp.float32, -lim2, lim2)}
    _L0_ffn_all = _L0_ffn_setup()
    _L0_ffn_in = {k: v for k, v in _L0_ffn_all.items() if k in ('w1', 'conv_w', 'conv_b', 'w2')}
    del _L0_ffn_all

    def _L1_attn_setup():
        import jax, jax.numpy as jnp
        import numpy as np
        EPS = 1e-05

        def rmsnorm(x, w):
            return x * jax.lax.rsqrt(jnp.mean(x * x, axis=-1, keepdims=True) + EPS) * w

        def depthwise_conv1d(x, w, b):
            k = w.shape[-1]
            p = (k - 1) // 2
            y = jax.lax.conv_general_dilated(x, w, window_strides=(1,), padding=[(p, p)], feature_group_count=x.shape[1], dimension_numbers=('NCH', 'OIH', 'NCH'))
            return y + b[None, :, None]

        def selective_scan(u, delta, A, B, C, D):

            def step(h, inp):
                d_t, B_t, C_t, u_t = inp
                dA = jnp.exp(d_t[..., None] * A)
                h = dA * h + (d_t * u_t)[..., None] * B_t[:, None, :]
                y = jnp.einsum('bdn,bn->bd', h, C_t)
                return (h, y)
            b, l, d_in = u.shape
            n = A.shape[1]
            h0 = jnp.zeros((b, d_in, n), u.dtype)
            xs = (jnp.moveaxis(delta, 1, 0), jnp.moveaxis(B, 1, 0), jnp.moveaxis(C, 1, 0), jnp.moveaxis(u, 1, 0))
            _, ys = jax.lax.scan(step, h0, xs)
            return jnp.moveaxis(ys, 0, 1) + u * D

        def mamba_block(x, Wi, bi, cw, cb, Wx, Wdt, bdt, A_log, D, Wo, bo, dt_rank, n):
            d_inner = A_log.shape[0]
            xr = x @ Wi.T + bi
            xs, res = jnp.split(xr, 2, axis=-1)
            xs = depthwise_conv1d(jnp.swapaxes(xs, 1, 2), cw, cb)
            xs = jax.nn.silu(jnp.swapaxes(xs, 1, 2))
            x_dbl = xs @ Wx.T
            dlt, B, C = jnp.split(x_dbl, [dt_rank, dt_rank + n], axis=-1)
            delta = jax.nn.softplus(dlt @ Wdt.T + bdt)
            A = -jnp.exp(A_log)
            y = selective_scan(xs, delta, A, B, C, D)
            y = y * jax.nn.silu(res)
            return y @ Wo.T + bo
        key = jax.random.key(seed)
        L, b, l, d, di, n, dtr, k = (2, 4, 256, 256, 512, 16, 64, 5)
        ks = jax.random.split(key, 12)
        s = lambda kk, shape, scale: jax.random.normal(kk, shape, jnp.float32) * scale
        inp = {'x': s(ks[0], (b, l, d), 1.0), 'in_proj_w': s(ks[1], (L, 2 * di, d), d ** (-0.5)), 'in_proj_b': s(ks[2], (L, 2 * di), 0.02), 'conv_w': s(ks[3], (L, di, 1, k), k ** (-0.5)), 'conv_b': s(ks[4], (L, di), 0.02), 'x_proj_w': s(ks[5], (L, dtr + 2 * n, di), di ** (-0.5)), 'dt_proj_w': s(ks[6], (L, di, dtr), dtr ** (-0.5)), 'dt_proj_b': s(ks[7], (L, di), 0.02), 'A_log': jnp.broadcast_to(jnp.log(jnp.arange(1, n + 1, dtype=jnp.float32)), (L, di, n)) * 1.0, 'D': jnp.ones((L, di), jnp.float32), 'out_proj_w': s(ks[8], (L, d, di), di ** (-0.5)), 'out_proj_b': s(ks[9], (L, d), 0.02), 'norm_w': jnp.ones((L, d), jnp.float32), 'norm_f_w': jnp.ones((d,), jnp.float32)}
        return inp
    _L1_attn_all = _L1_attn_setup()
    _L1_attn_in = {k: v for k, v in _L1_attn_all.items() if k in ('in_proj_w', 'in_proj_b', 'conv_w', 'conv_b', 'x_proj_w', 'dt_proj_w', 'dt_proj_b', 'A_log', 'D', 'out_proj_w', 'out_proj_b', 'norm_w', 'norm_f_w')}
    del _L1_attn_all

    def _L1_xattn_setup():
        import jax, jax.numpy as jnp
        import numpy as np
        B, S, H, NH = (2, 512, 256, 16)
        HD = H // NH
        key = jax.random.key(seed)
        ks = jax.random.split(key, 12)
        inp = {'query': jax.random.normal(ks[0], (B, S, H), dtype=jnp.float32), 'key': jax.random.normal(ks[1], (B, S, H), dtype=jnp.float32), 'value': jax.random.normal(ks[2], (B, S, H), dtype=jnp.float32), 'mask': jnp.ones((B, 1, S, S), dtype=jnp.int32), 'script_mask': jax.random.uniform(ks[3], (B, S, S), dtype=jnp.float32)}
        scale = 1.0 / np.sqrt(H)
        inp['Wq'] = jax.random.normal(ks[4], (H, H), dtype=jnp.float32) * scale
        inp['bq'] = jnp.zeros((H,), dtype=jnp.float32)
        inp['Wk'] = jax.random.normal(ks[5], (H, H), dtype=jnp.float32) * scale
        inp['bk'] = jnp.zeros((H,), dtype=jnp.float32)
        inp['Wv'] = jax.random.normal(ks[6], (H, H), dtype=jnp.float32) * scale
        inp['bv'] = jnp.zeros((H,), dtype=jnp.float32)
        inp['Wo'] = jax.random.normal(ks[7], (H, H), dtype=jnp.float32) * scale
        inp['bo'] = jnp.zeros((H,), dtype=jnp.float32)
        return inp
    _L1_xattn_all = _L1_xattn_setup()
    _L1_xattn_in = {k: v for k, v in _L1_xattn_all.items() if k in ('Wq', 'bq', 'Wk', 'bk', 'Wv', 'bv', 'Wo', 'bo')}
    del _L1_xattn_all

    def _L1_ffn_setup():
        import jax, jax.numpy as jnp
        import numpy as np
        BS, L, D = (4, 512, 256)
        H, E, K = (8, 16, 2)
        HD = D // H
        I = 1024 // H
        key = jax.random.key(seed)
        ks = jax.random.split(key, 10)
        s = lambda k, shp, fan: jax.random.normal(k, shp, jnp.float32) / np.sqrt(fan)
        return {'x': jax.random.normal(ks[0], (BS, L, D), jnp.float32), 'Wm': s(ks[1], (D, D), D), 'bm': jnp.zeros((D,), jnp.float32), 'expert_emb': jax.random.normal(ks[2], (HD, E), jnp.float32), 'W1': s(ks[3], (E, HD, I), HD), 'b1': jnp.zeros((E, I), jnp.float32), 'W2': s(ks[4], (E, I, HD), I), 'b2': jnp.zeros((E, HD), jnp.float32), 'Wo': s(ks[5], (D, D), D), 'bo': jnp.zeros((D,), jnp.float32)}
    _L1_ffn_all = _L1_ffn_setup()
    _L1_ffn_in = {k: v for k, v in _L1_ffn_all.items() if k in ('Wm', 'bm', 'expert_emb', 'W1', 'b1', 'W2', 'b2', 'Wo', 'bo')}
    del _L1_ffn_all
    return {'x': x, 'ctx_1024': ctx_1024, 'fside_BxSxS2_0': fside_BxSxS2_0, 'mask_Bx1xSxS2_if1': mask_Bx1xSxS2_if1, 'L0_attn_w_qkv': _L0_attn_in['w_qkv'], 'L0_attn_w_proj': _L0_attn_in['w_proj'], 'L0_xattn_Wq': _L0_xattn_in['Wq'], 'L0_xattn_bq': _L0_xattn_in['bq'], 'L0_xattn_Wk': _L0_xattn_in['Wk'], 'L0_xattn_bk': _L0_xattn_in['bk'], 'L0_xattn_Wv': _L0_xattn_in['Wv'], 'L0_xattn_bv': _L0_xattn_in['bv'], 'L0_xattn_Wo': _L0_xattn_in['Wo'], 'L0_xattn_bo': _L0_xattn_in['bo'], 'L0_ffn_w1': _L0_ffn_in['w1'], 'L0_ffn_conv_w': _L0_ffn_in['conv_w'], 'L0_ffn_conv_b': _L0_ffn_in['conv_b'], 'L0_ffn_w2': _L0_ffn_in['w2'], 'L1_attn_in_proj_w': _L1_attn_in['in_proj_w'], 'L1_attn_in_proj_b': _L1_attn_in['in_proj_b'], 'L1_attn_conv_w': _L1_attn_in['conv_w'], 'L1_attn_conv_b': _L1_attn_in['conv_b'], 'L1_attn_x_proj_w': _L1_attn_in['x_proj_w'], 'L1_attn_dt_proj_w': _L1_attn_in['dt_proj_w'], 'L1_attn_dt_proj_b': _L1_attn_in['dt_proj_b'], 'L1_attn_A_log': _L1_attn_in['A_log'], 'L1_attn_D': _L1_attn_in['D'], 'L1_attn_out_proj_w': _L1_attn_in['out_proj_w'], 'L1_attn_out_proj_b': _L1_attn_in['out_proj_b'], 'L1_attn_norm_w': _L1_attn_in['norm_w'], 'L1_attn_norm_f_w': _L1_attn_in['norm_f_w'], 'L1_xattn_Wq': _L1_xattn_in['Wq'], 'L1_xattn_bq': _L1_xattn_in['bq'], 'L1_xattn_Wk': _L1_xattn_in['Wk'], 'L1_xattn_bk': _L1_xattn_in['bk'], 'L1_xattn_Wv': _L1_xattn_in['Wv'], 'L1_xattn_bv': _L1_xattn_in['bv'], 'L1_xattn_Wo': _L1_xattn_in['Wo'], 'L1_xattn_bo': _L1_xattn_in['bo'], 'L1_ffn_Wm': _L1_ffn_in['Wm'], 'L1_ffn_bm': _L1_ffn_in['bm'], 'L1_ffn_expert_emb': _L1_ffn_in['expert_emb'], 'L1_ffn_W1': _L1_ffn_in['W1'], 'L1_ffn_b1': _L1_ffn_in['b1'], 'L1_ffn_W2': _L1_ffn_in['W2'], 'L1_ffn_b2': _L1_ffn_in['b2'], 'L1_ffn_Wo': _L1_ffn_in['Wo'], 'L1_ffn_bo': _L1_ffn_in['bo']}

def reference(x, ctx_1024, fside_BxSxS2_0, mask_Bx1xSxS2_if1, L0_attn_w_qkv, L0_attn_w_proj, L0_xattn_Wq, L0_xattn_bq, L0_xattn_Wk, L0_xattn_bk, L0_xattn_Wv, L0_xattn_bv, L0_xattn_Wo, L0_xattn_bo, L0_ffn_w1, L0_ffn_conv_w, L0_ffn_conv_b, L0_ffn_w2, L1_attn_in_proj_w, L1_attn_in_proj_b, L1_attn_conv_w, L1_attn_conv_b, L1_attn_x_proj_w, L1_attn_dt_proj_w, L1_attn_dt_proj_b, L1_attn_A_log, L1_attn_D, L1_attn_out_proj_w, L1_attn_out_proj_b, L1_attn_norm_w, L1_attn_norm_f_w, L1_xattn_Wq, L1_xattn_bq, L1_xattn_Wk, L1_xattn_bk, L1_xattn_Wv, L1_xattn_bv, L1_xattn_Wo, L1_xattn_bo, L1_ffn_Wm, L1_ffn_bm, L1_ffn_expert_emb, L1_ffn_W1, L1_ffn_b1, L1_ffn_W2, L1_ffn_b2, L1_ffn_Wo, L1_ffn_bo):
    import jax
    import jax.numpy as jnp

    def _L0_attn_ref(x, w_qkv, w_proj):
        import jax, jax.numpy as jnp
        import numpy as np
        D = 256
        H = 16
        DH = D // H
        B, L, _ = x.shape
        qkv = x @ w_qkv.T
        q, k, v = jnp.split(qkv, 3, axis=-1)
        q = q.reshape(B, L, H, DH)
        k = k.reshape(B, L, H, DH)
        v = v.reshape(B, L, H, DH)
        scale = 1.0 / np.sqrt(DH)
        scores = jnp.einsum('blhd,bmhd->bhlm', q, k) * scale
        causal = jnp.arange(L)[:, None] < jnp.arange(L)[None, :]
        scores = jnp.where(causal[None, None, :, :], -jnp.inf, scores)
        att = jax.nn.softmax(scores, axis=-1)
        out = jnp.einsum('bhlm,bmhd->blhd', att, v)
        out = out.reshape(B, L, D)
        return out @ w_proj.T

    def _L0_xattn_ref(x, l, Wq, bq, Wk, bk, Wv, bv, Wo, bo):
        import jax, jax.numpy as jnp
        import numpy as np
        DIM = 256
        HEADS = 16
        DS = 4
        B, N, _ = l.shape
        M = x.shape[1]
        d = DIM // HEADS

        def split_heads(t):
            return t.reshape(t.shape[0], t.shape[1], HEADS, d).transpose(0, 2, 1, 3)
        q = split_heads(l @ Wq.T + bq)
        k = split_heads(x @ Wk.T + bk)
        v = split_heads(x @ Wv.T + bv)
        scores = jnp.einsum('bhid,bhjd->bhij', q, k) * d ** (-0.5)
        ii = jnp.arange(N)[:, None]
        jj = jnp.arange(M)[None, :]
        allowed = jj // DS <= ii
        scores = jnp.where(allowed[None, None], scores, -jnp.inf)
        attn = jax.nn.softmax(scores, axis=-1)
        out = jnp.einsum('bhij,bhjd->bhid', attn, v)
        out = out.transpose(0, 2, 1, 3).reshape(B, N, DIM)
        return out @ Wo.T + bo

    def _L0_ffn_ref(x, w1, conv_w, conv_b, w2):
        import jax, jax.numpy as jnp
        import numpy as np
        B, S, D_MODEL, D_HIDDEN = (4, 512, 256, 1024)

        def act_quant(x):
            scale = 127.0 / jnp.clip(jnp.max(jnp.abs(x), axis=-1, keepdims=True), 1e-05)
            return jnp.clip(jnp.round(x * scale), -128, 127) / scale

        def weight_quant(w):
            scale = 1.0 / jnp.clip(jnp.mean(jnp.abs(w)), 1e-05)
            return jnp.clip(jnp.round(w * scale), -1, 1) / scale

        def bit_linear(x, w):
            xq = x + jax.lax.stop_gradient(act_quant(x) - x)
            wq = w + jax.lax.stop_gradient(weight_quant(w) - w)
            return jnp.einsum('bsd,hd->bsh', xq, wq)

        def depthwise_conv1d(x_bcl, w, b):
            y = jax.lax.conv_general_dilated(x_bcl, w, window_strides=(1,), padding=[(1, 1)], dimension_numbers=('NCH', 'OIH', 'NCH'), feature_group_count=x_bcl.shape[1])
            return y + b[None, :, None]
        h = bit_linear(x, w1)
        h = depthwise_conv1d(h.transpose(0, 2, 1), conv_w, conv_b)
        h = h.transpose(0, 2, 1)
        h = jax.nn.silu(h)
        return bit_linear(h, w2)

    def _L1_attn_ref(x, in_proj_w, in_proj_b, conv_w, conv_b, x_proj_w, dt_proj_w, dt_proj_b, A_log, D, out_proj_w, out_proj_b, norm_w, norm_f_w):
        import jax, jax.numpy as jnp
        import numpy as np
        EPS = 1e-05

        def rmsnorm(x, w):
            return x * jax.lax.rsqrt(jnp.mean(x * x, axis=-1, keepdims=True) + EPS) * w

        def depthwise_conv1d(x, w, b):
            k = w.shape[-1]
            p = (k - 1) // 2
            y = jax.lax.conv_general_dilated(x, w, window_strides=(1,), padding=[(p, p)], feature_group_count=x.shape[1], dimension_numbers=('NCH', 'OIH', 'NCH'))
            return y + b[None, :, None]

        def selective_scan(u, delta, A, B, C, D):

            def step(h, inp):
                d_t, B_t, C_t, u_t = inp
                dA = jnp.exp(d_t[..., None] * A)
                h = dA * h + (d_t * u_t)[..., None] * B_t[:, None, :]
                y = jnp.einsum('bdn,bn->bd', h, C_t)
                return (h, y)
            b, l, d_in = u.shape
            n = A.shape[1]
            h0 = jnp.zeros((b, d_in, n), u.dtype)
            xs = (jnp.moveaxis(delta, 1, 0), jnp.moveaxis(B, 1, 0), jnp.moveaxis(C, 1, 0), jnp.moveaxis(u, 1, 0))
            _, ys = jax.lax.scan(step, h0, xs)
            return jnp.moveaxis(ys, 0, 1) + u * D

        def mamba_block(x, Wi, bi, cw, cb, Wx, Wdt, bdt, A_log, D, Wo, bo, dt_rank, n):
            d_inner = A_log.shape[0]
            xr = x @ Wi.T + bi
            xs, res = jnp.split(xr, 2, axis=-1)
            xs = depthwise_conv1d(jnp.swapaxes(xs, 1, 2), cw, cb)
            xs = jax.nn.silu(jnp.swapaxes(xs, 1, 2))
            x_dbl = xs @ Wx.T
            dlt, B, C = jnp.split(x_dbl, [dt_rank, dt_rank + n], axis=-1)
            delta = jax.nn.softplus(dlt @ Wdt.T + bdt)
            A = -jnp.exp(A_log)
            y = selective_scan(xs, delta, A, B, C, D)
            y = y * jax.nn.silu(res)
            return y @ Wo.T + bo
        n = A_log.shape[-1]
        dt_rank = x_proj_w.shape[1] - 2 * n
        h = x
        for i in range(in_proj_w.shape[0]):
            h = h + mamba_block(rmsnorm(h, norm_w[i]), in_proj_w[i], in_proj_b[i], conv_w[i], conv_b[i], x_proj_w[i], dt_proj_w[i], dt_proj_b[i], A_log[i], D[i], out_proj_w[i], out_proj_b[i], dt_rank, n)
        return rmsnorm(h, norm_f_w)

    def _L1_xattn_ref(query, key, value, mask, script_mask, Wq, bq, Wk, bk, Wv, bv, Wo, bo):
        import jax, jax.numpy as jnp
        import numpy as np
        B, S, H, NH = (2, 512, 256, 16)
        HD = H // NH
        b, s, h = query.shape
        q = (query @ Wq.T + bq).reshape(b, s, NH, HD).transpose(0, 2, 1, 3)
        k = (key @ Wk.T + bk).reshape(b, s, NH, HD).transpose(0, 2, 1, 3)
        v = (value @ Wv.T + bv).reshape(b, s, NH, HD).transpose(0, 2, 1, 3)
        scores = jnp.einsum('bhqd,bhkd->bhqk', q, k) / jnp.sqrt(jnp.float32(HD))
        scores = scores * script_mask[:, None, :, :]
        scores = jnp.where(mask == 0, -jnp.inf, scores)
        attn = jax.nn.softmax(scores, axis=-1)
        out = jnp.einsum('bhqk,bhkd->bhqd', attn, v)
        out = out.transpose(0, 2, 1, 3).reshape(b, s, h)
        return out @ Wo.T + bo

    def _L1_ffn_ref(x, Wm, bm, expert_emb, W1, b1, W2, b2, Wo, bo):
        import jax, jax.numpy as jnp
        import numpy as np
        BS, L, D = (4, 512, 256)
        H, E, K = (8, 16, 2)
        HD = D // H
        I = 1024 // H
        bs, L_, d = x.shape
        h = x @ Wm + bm
        t = h.reshape(bs * L_ * H, HD)
        logits = t @ expert_emb
        w = jax.nn.softmax(logits, axis=-1)
        topw, topi = jax.lax.top_k(w, K)
        hmid = jax.nn.gelu(jnp.einsum('td,edi->tei', t, W1) + b1, approximate=False)
        eo = jnp.einsum('tei,eio->teo', hmid, W2) + b2
        sel = jnp.take_along_axis(eo, topi[:, :, None], axis=1)
        comb = (sel * topw[:, :, None]).sum(axis=1)
        out = comb.reshape(bs, L_, d)
        return out @ Wo + bo
    x = x + _L0_attn_ref(_layernorm(x, axis=-1), L0_attn_w_qkv, L0_attn_w_proj)
    x = x + _L0_xattn_ref(ctx_1024, _layernorm(x, axis=-1), L0_xattn_Wq, L0_xattn_bq, L0_xattn_Wk, L0_xattn_bk, L0_xattn_Wv, L0_xattn_bv, L0_xattn_Wo, L0_xattn_bo)
    x = x + _L0_ffn_ref(_layernorm(x, axis=-1), L0_ffn_w1, L0_ffn_conv_w, L0_ffn_conv_b, L0_ffn_w2)
    x = x + _L1_attn_ref(_layernorm(x, axis=-1), L1_attn_in_proj_w, L1_attn_in_proj_b, L1_attn_conv_w, L1_attn_conv_b, L1_attn_x_proj_w, L1_attn_dt_proj_w, L1_attn_dt_proj_b, L1_attn_A_log, L1_attn_D, L1_attn_out_proj_w, L1_attn_out_proj_b, L1_attn_norm_w, L1_attn_norm_f_w)
    x = x + _L1_xattn_ref(_layernorm(x, axis=-1), ctx_1024, ctx_1024, mask_Bx1xSxS2_if1, fside_BxSxS2_0, L1_xattn_Wq, L1_xattn_bq, L1_xattn_Wk, L1_xattn_bk, L1_xattn_Wv, L1_xattn_bv, L1_xattn_Wo, L1_xattn_bo)
    x = x + _L1_ffn_ref(_layernorm(x, axis=-1), L1_ffn_Wm, L1_ffn_bm, L1_ffn_expert_emb, L1_ffn_W1, L1_ffn_b1, L1_ffn_W2, L1_ffn_b2, L1_ffn_Wo, L1_ffn_bo)
    return x

_drawn_inputs = setup_inputs


def setup_inputs(seed=0):
    import zlib

    import numpy as np

    out = dict(_drawn_inputs(seed))
    spreads = {'L0_xattn_bq': (0.0, 0.8),
     'L0_xattn_bk': (0.0, 0.8),
     'L0_xattn_bv': (0.0, 0.1),
     'L0_xattn_bo': (0.0, 0.1),
     'L1_attn_D': (1.0, 0.2),
     'L1_attn_norm_w': (1.0, 0.2),
     'L1_attn_norm_f_w': (1.0, 0.2),
     'L1_xattn_bq': (0.0, 0.8),
     'L1_xattn_bk': (0.0, 0.8),
     'L1_xattn_bv': (0.0, 0.1),
     'L1_xattn_bo': (0.0, 0.1),
     'L1_ffn_bm': (0.0, 0.1),
     'L1_ffn_b1': (0.0, 0.282),
     'L1_ffn_b2': (0.0, 0.1),
     'L1_ffn_bo': (0.0, 0.1)}
    factors = {'fside_BxSxS2_0': 2.898,
     'L0_xattn_Wq': 8.0,
     'L0_xattn_Wk': 8.0,
     'L1_attn_in_proj_b': 2.932,
     'L1_attn_conv_b': 3.351,
     'L1_attn_dt_proj_b': 8.0,
     'L1_attn_out_proj_b': 3.197}
    for name, (base, spread) in spreads.items():
        noise = np.random.default_rng([zlib.crc32(name.encode()), seed]).standard_normal(out[name].shape)
        drawn = base * np.exp(spread * noise) if base else spread * noise
        out[name] = jnp.asarray(drawn.astype(out[name].dtype))
    for name, factor in factors.items():
        out[name] = (out[name] * factor).astype(out[name].dtype)
    return out
```

```python
from contextlib import ExitStack

import concourse.bass as bass
from concourse import mybir

ALU = mybir.AluOpType
ACT = mybir.ActivationFunctionType
F32 = mybir.dt.float32
BF16 = mybir.dt.bfloat16
I32 = mybir.dt.int32
AX = mybir.AxisListType

P = 128
B, S, D = 8, 256, 256
PAIR = 2
TURNS = B // PAIR
TOK = PAIR * S
TT = TOK // P
KD = D // P
HEADS, DH = 16, 16
QUADS = HEADS // 4
GROUPS = TT * QUADS
POOL_QUAD = QUADS - 1
HID = 1024
MH = HID // P
DI, NS, DTR, TAPS = 512, 16, 64, 5
DT = DI // P
NC = 2
CHUNKS = NS // NC
STEPS = CHUNKS * DT
BC3 = 3 * 2 * NS
MHD, EXP, EH = 8, 16, 128
MD = D // MHD
EPS = 1e-5
ROUND = 12582912.0

SMALL = ([(f"b_qk{n}", (2, KD)) for n in (1, 2)] + [("conv3_w", (MH, 3)), ("conv3_b", (MH,))]
         + [(name + str(l), shape) for l in range(2)
            for name, shape in [("b_in", (2 * DT,)), ("conv5_w", (DT, TAPS)), ("conv5_b", (DT,)), ("b_dt", (DT,)),
                                ("decay", (DT, NS)), ("skip", (DT,)), ("norm_w", (KD,))]]
         + [("b_m", (KD,)), ("b_e1", (EXP,)), ("head_rows", (8,)), ("rank", (EXP,)), ("minus_part", (2,))])
BIAS_ROWS = ["L0_xattn_bv", "L0_xattn_bo", "L1_xattn_bv", "L1_xattn_bo", "out_b0", "out_b1", "L1_ffn_bo"]


LASTING = """
    const_loaded ternary_loaded attn_w_loaded rest_w_loaded   (weights and constants are in SBUF)
    dve_setup half_set w_sum_ready w_sum_ps decay_exp ternary_ready setup_done   (steps before the loop)
    x_loaded ctx_loaded side_loaded   (a turn's rows are in SBUF)
    stored   (a turn's result is in DRAM)
    turn_opened   (the semaphores of the turn before have been cleared)
"""
IN_TURN = """
    x_in_used ctx_in_used side_used   (a turn's rows have been read: the next may be loaded)
    x_done turn_ended
    act_order dve_order   (an engine waits for its own results)
    var_ready rstd_ready xn_ready   (normalisation)
    flip_ps flip_sb   (token-major to feature-major)
    qkv_ps q_sb k_sb k_masked k_masked_pool v_zeroed v_sb scores_ps scaled_ready masked_ready max_ready probs_ready probsT_ps probsT_sb pv_done
    inverse_ready oT_ready res_ps   (attention; res_ps: what is added to the residual rows)
    q8_ready q8T_ps q8T_sb diag_ready back_ps back_sb up_ps up_sb conv_mid conv3_done act_ready actT_ps
    scale2_ready rounded_ready q8h_ready q8hT_ps q8hT_sb down_ps   (convolution MLP)
    in_ps in_sb conv5_done xs_ready xdbl_ps low_rank_sb bc_sb bc_split dt_ps ln_ready delta_ready bc_ps b_bc_ready
    c_bc_ready dA_heads dA_ready injected h_ready hc_ready y_added y_ready   (Mamba)
    t_ps t_sb t_zeroed t_head_sb logits_ps logits_ready router_exp gates_ready gatesT_ps gatesT_sb gates_split b2_ps acc_set
    gate_ps gate_sb up_e_ps hmid_ready down_e_done prod_ready acc_added   (mixture of experts)
"""


def names_in(text):
    return " ".join(piece.split(")")[-1] for piece in text.split("(")).split()


def program(nc, a, out):
    with ExitStack() as ctx:
        def sb(name, shape, dt=F32):
            return ctx.enter_context(nc.sbuf_tensor(name, shape, dt))

        sem = {name: ctx.enter_context(nc.semaphore(name)) for name in names_in(IN_TURN) + names_in(LASTING)}
        in_turn = [sem[name].num for name in names_in(IN_TURN)]
        assert in_turn == list(range(in_turn[0], in_turn[0] + len(in_turn)))

        def end_turn(eng, turn):
            eng.nop().then_inc(sem["turn_ended"], 1)
            eng.wait_ge(sem["turn_opened"], turn + 1)

        ps = ctx.enter_context(nc.psum_tensor("ps", [P, 8, 512], F32))

        ident = sb("ident", [P, P])
        ident_bf = sb("ident_bf", [P, P], BF16)
        causal_bf = sb("causal_bf", [P, P], BF16)
        window_bf = sb("window_bf", [P, S], BF16)
        same_of_three = sb("same_of_three", [P, 2 * NS], BF16)
        ones = sb("ones", [P, P])
        magic = sb("magic", [P, 1])
        minus_half = sb("minus_half", [P, TT])
        bias_rows = sb("bias_rows", [P, 2, D])

        def cells(shape):
            n = 1
            for s_ in shape:
                n *= s_
            return n

        small = sb("small", [P, sum(cells(shape) for _, shape in SMALL)])
        table, at_ = {}, 0
        for name_, shape in SMALL:
            ap = small[:, at_:at_ + cells(shape)]
            table[name_] = ap if len(shape) == 1 else ap.rearrange("p (a b) -> p a b", b=shape[1])
            at_ += cells(shape)
        b_qk = {n: table[f"b_qk{n}"] for n in (1, 2)}
        conv3_w, conv3_b = table["conv3_w"], table["conv3_b"]
        b_in, conv5_w, conv5_b, b_dt, decay, skip, norm_w = (
            [table[name_ + str(l)] for l in range(2)]
            for name_ in ("b_in", "conv5_w", "conv5_b", "b_dt", "decay", "skip", "norm_w"))
        b_m, b_e1 = table["b_m"], table["b_e1"]
        head_rows = table["head_rows"]
        minus_part = table["minus_part"]
        rank = table["rank"]

        w_qkv = sb("w_qkv", [P, KD, 3 * D])
        w_attn = {(0, "o"): sb("w_proj", [P, KD, D])}
        for n in (1, 2):
            for c in "qkvo":
                w_attn[n, c] = sb(f"w_{c}{n}", [P, KD, D])
        w_up = sb("w_up", [P, KD, HID], BF16)
        w_down = sb("w_down", [P, MH, D], BF16)
        unquant = sb("unquant", [P, 2])
        w_in = [sb(f"w_in{l}", [P, KD, 2 * DI]) for l in range(2)]
        w_x = [sb(f"w_x{l}", [P, DT, DTR + BC3]) for l in range(2)]
        w_dt = [sb(f"w_dt{l}", [DTR, DI]) for l in range(2)]
        w_out = [sb(f"w_out{l}", [P, DT, D]) for l in range(2)]
        norm_f = sb("norm_f", [P, D])
        w_m = sb("w_m", [P, KD, D])
        emb = sb("emb", [P, 4 * EXP])
        w_e1 = sb("w_e1", [P, EXP, EH])
        w_e2 = sb("w_e2", [P, EXP, MD])
        b_e2 = sb("b_e2", [P, KD, P])
        w_mo = sb("w_mo", [P, KD, D])
        gate_sel = sb("gate_sel", [P, EXP * KD, P], BF16)

        x_in = sb("x_in", [P, TT, D])
        ctx_in = sb("ctx_in", [P, TT, D])
        side = sb("side", [P, TT, S])
        mask_in = sb("mask_in", [P, TT, S], I32)
        x = sb("x", [P, TT, D])
        xn = sb("xn", [P, TT, D])
        h_res = sb("h_res", [P, TT, D])
        xT = sb("xT", [P, KD, TOK])
        ctxT = sb("ctxT", [P, KD, TOK])
        stats = sb("stats", [P, TT, 6])
        mean_var = sb("mean_var", [P, TT, 2])
        sq = sb("sq", [P, TT])
        var_eps = sb("var_eps", [P, TT])
        rstd = sb("rstd", [P, TT])

        REGION = 19648
        region = sb("region", [P, REGION])
        taken = [0]

        def part(shape, dt=F32):
            n = 1
            for s_ in shape:
                n *= s_
            words = n if dt != BF16 else n // 2
            at = taken[0]
            taken[0] += words
            assert taken[0] <= REGION, taken[0]
            ap = region[:, at:at + words]
            if dt == BF16:
                ap = ap.bitcast(BF16)
            names = "abcd"[:len(shape)]
            if len(shape) > 1:
                ap = ap.rearrange(f"p ({' '.join(names)}) -> p {' '.join(names)}",
                                  **{c: s_ for c, s_ in zip(names[1:], shape[1:])})
            return ap

        taken[0] = 0
        qT = part([KD, TOK])
        kT = [part([KD, TOK]) for _ in range(P // DH)]
        v_sb = [part([TT, D]) for _ in range(2)]
        probs = [part([4, S]) for _ in range(2)]
        probsT = [part([2, 4 * P]) for _ in range(2)]
        oT_sb = part([KD, TOK])
        k_all = oT_sb
        scaled = [part([4, S]) for _ in range(3)]
        neg_max = part([TT, HEADS])
        row_sum = part([TT, HEADS])
        row_rec = part([TT, HEADS])
        taken[0] = 0
        q8 = part([TT, D], BF16)
        q8T = part([KD, TOK], BF16)
        absmax = part([TT])
        q_scale = part([TT])
        q_back = part([TT])
        diag = part([TT, P])
        back_rows = part([TOK])
        up = [part([TOK]) for _ in range(2)]
        act = part([MH, TOK])
        rounded = [part([HID]) for _ in range(2)]
        q8h = [part([HID], BF16) for _ in range(2)]
        q8hT = [part([MH, P], BF16) for _ in range(2)]
        taken[0] = 0
        w_up_f = part([KD, HID])
        w_down_f = part([MH, D])
        w_sum = part([2])
        w_scale = part([2])
        causal_f = part([P])
        window_f = part([S])
        gate_sel_f = part([EXP * KD, P])
        taken[0] = 0
        xp = part([DT, TOK])
        gate_res = part([DT, TOK])
        xs = part([DT, TOK])
        delta = part([DT, TOK])
        du = part([DT, TOK])
        dA = [part([NC, TOK]) for _ in range(2)]
        hbuf = [part([NC, TOK]) for _ in range(3)]
        b_bc = [part([NC, TOK]) for _ in range(2)]
        c_bc = [part([NC, TOK]) for _ in range(2)]
        low_rank = xT[:, 0, :]
        bc_rest = xT[:, 1, :]
        both = xn[:].rearrange("p t d -> p (t d)").bitcast(BF16)
        bc, bc_round = both[:, 0:TOK], both[:, TOK:2 * TOK]
        taken[0] = 0
        tT = part([KD, TOK])
        tT_head = [part([KD, TOK]) for _ in range(4)]
        lg = part([TT * MHD, EXP])
        pr = part([TT * MHD, EXP])
        pick = part([TT * MHD, EXP])
        first = part([TT * MHD, EXP])
        left = part([TT * MHD, EXP])
        best = part([TT * MHD])
        z_sum = part([TT * MHD])
        gates = part([TT, MHD * EXP])
        gatesT = part([TOK])
        gates_rest = part([TOK])
        gates_part = [part([TOK], BF16) for _ in range(3)]
        hmid = [part([4, TOK]) for _ in range(2)]
        gate_bc = [part([TOK]) for _ in range(2)]
        prod = [part([TOK]) for _ in range(2)]
        acc = part([KD, TOK])

        block = ctx.enter_context(nc.Block())

        def of(k, t):
            return slice(t * P, (t + 1) * P)

        def attn_shape(n, tt):
            return 1 if n == 0 and tt % 2 == 0 else 2

        def halves(t):
            return t[:].rearrange("p (g h) d -> p g h d", g=PAIR)

        @block.sync
        def _(sp):
            def load(dst, src, name):
                sp.dma_start(dst, src).then_inc(sem[name], 16)

            def cols(name):
                return a[name].rearrange("(k p) n -> p k n", p=P)

            for dst, name in [(ident[:], "c_ident"), (causal_f, "c_causal"), (window_f, "c_window"),
                              (gate_sel_f, "c_gate_sel"), (small[:], "small")]:
                load(dst, a[name], "const_loaded")
            load(w_up_f, cols("w1T"), "ternary_loaded")
            load(w_down_f, cols("w2T"), "ternary_loaded")
            load(w_qkv[:], cols("qkvT"), "attn_w_loaded")
            load(w_attn[0, "o"][:], cols("projT"), "attn_w_loaded")
            for n in (1, 2):
                for c in "qkvo":
                    load(w_attn[n, c][:], cols(f"x{n}_{c}T"), "attn_w_loaded")
            for i, name in enumerate(BIAS_ROWS):
                r = 32 * (i % 4)
                load(bias_rows[r:r + 1, i // 4, :], a[name], "attn_w_loaded")
            for l in range(2):
                load(w_in[l][:], cols(f"inT{l}"), "rest_w_loaded")
                load(w_x[l][:], cols(f"xT{l}"), "rest_w_loaded")
                load(w_dt[l][:], a[f"dtT{l}"], "rest_w_loaded")
                load(w_out[l][:], cols(f"outT{l}"), "rest_w_loaded")
            load(norm_f[:], a["norm_f"].partition_broadcast(P), "rest_w_loaded")
            load(w_m[:], cols("Wm"), "rest_w_loaded")
            load(emb[:], a["emb"], "rest_w_loaded")
            for j in range(4):
                load(w_e1[32 * j:32 * j + 32, :, :], a["W1"].rearrange("e d i -> d e i"), "rest_w_loaded")
            load(w_e2[:], a["W2"].rearrange("e i o -> i e o"), "rest_w_loaded")
            load(b_e2[:], a["b2_rows"].rearrange("k p m -> p k m"), "rest_w_loaded")
            load(w_mo[:], cols("Wo"), "rest_w_loaded")

            x_v = a["x"].rearrange("(n g) (h p) d -> n p g h d", g=PAIR, p=P)
            ctx_v = a["ctx"].rearrange("(n g) (h p) d -> n p g h d", g=PAIR, p=P)
            side_v = a["side"].rearrange("(n g) (h p) d -> n p g h d", g=PAIR, p=P)
            mask_v = a["mask"].rearrange("(n g) (h p) d -> n p g h d", g=PAIR, p=P)
            def load_ctx(turn):
                for g in range(PAIR):
                    sp.dma_start(halves(ctx_in)[:, g], ctx_v[turn, :, g]).then_inc(sem["ctx_loaded"], 16)

            def load_x(turn):
                for g in range(PAIR):
                    sp.dma_start(halves(x_in)[:, g], x_v[turn, :, g]).then_inc(sem["x_loaded"], 16)

            def load_side(turn):
                for g in range(PAIR):
                    sp.dma_start(halves(side)[:, g], side_v[turn, :, g]).then_inc(sem["side_loaded"], 16)
                    sp.dma_start(halves(mask_in)[:, g], mask_v[turn, :, g]).then_inc(sem["side_loaded"], 16)

            def run_turn(turn, more):
                sp.wait_ge(sem["ctx_in_used"], 1)
                if more:
                    load_ctx(turn + 1)
                sp.wait_ge(sem["x_in_used"], 1)
                if more:
                    load_x(turn + 1)
                sp.wait_ge(sem["side_used"], 1)
                if more:
                    load_side(turn + 1)
                sp.wait_ge(sem["x_done"], 1)
                sp.wait_ge(sem["turn_ended"], 4)
                sp.sem_clear(range(in_turn[0], in_turn[0] + len(in_turn)))
                sp.nop().then_inc(sem["turn_opened"], 1)

            load_ctx(0)
            load_x(0)
            load_side(0)
            with sp.Fori(0, TURNS - 1) as turn:
                run_turn(turn, True)
            run_turn(TURNS - 1, False)

        N_CONST, N_ATTN, N_REST = 5, 2 + 2 * 4 + len(BIAS_ROWS), 2 * 4 + 1 + 2 + 4 + 3

        @block.gpsimd
        def _(pool):
            pool.memset(minus_half[:], -0.5).then_inc(sem["half_set"], 1)
            pool.wait_ge(sem["half_set"], 1)
            pool.nop().then_inc(sem["stored"], 1)
            with pool.Fori(0, TURNS) as turn:
                def power(u):
                    pool.wait_ge(sem["var_ready"], u + 1)
                    pool.tensor_tensor(rstd[:], var_eps[:], minus_half[:], ALU.pow)\
                        .then_inc(sem["rstd_ready"], 1)

                def mask_keys(n):
                    for i in range(2):
                        pool.memset(v_sb[i].rearrange("p t (h o d) -> p (t h) o d", o=2, d=DH)[:, :, 1 - i], 0.0)\
                            .then_inc(sem["v_zeroed"], 1)
                    pool.wait_ge(sem["k_sb"], KD * (n + 1))
                    for i in range(4):
                        j = 4 + i
                        ins = pool.tensor_scalar(kT[j][:, KD - 1, :], k_all[:, KD - 1, :], head_rows[:, j:j + 1], None,
                                                 ALU.mult)
                    ins.then_inc(sem["k_masked_pool"], 1)

                power(0)
                mask_keys(0)
                power(1)
                mask_keys(1)
                power(2)
                power(3)
                for l in range(2):
                    power(4 + l)
                    for s in range(STEPS):
                        c = s // DT
                        pool.wait_ge(sem["h_ready"], l * STEPS + s + 1)
                        pool.tensor_tensor(hbuf[s % 3], hbuf[s % 3], c_bc[c % 2], ALU.mult)\
                            .then_inc(sem["hc_ready"], 1)
                power(6)
                power(7)
                mask_keys(2)
                for g in range(GROUPS):
                    pool.wait_ge(sem["scaled_ready"], g + 1)
                    keep = mask_in[:].bitcast(F32)[:, g // QUADS:g // QUADS + 1, :].to_broadcast([P, 4, S])
                    pool.tensor_tensor(scaled[g % 3], scaled[g % 3], keep, ALU.add)\
                        .then_inc(sem["masked_ready"], 1)
                power(8)
                for j in range(4):
                    pool.memset(tT_head[j], 0.0).then_inc(sem["t_zeroed"], 1)
                for v in range(EXP * KD):
                    pool.wait_ge(sem["prod_ready"], v + 1)
                    if v >= KD:
                        pool.wait_ge(sem["acc_added"], v - 1)
                    else:
                        pool.wait_ge(sem["acc_set"], v + 1)
                    pool.tensor_tensor(acc[:, v % KD, :], acc[:, v % KD, :], prod[v % 2], ALU.add)\
                        .then_inc(sem["acc_added"], 1)
                end_turn(pool, turn)

        @block.scalar
        def _(actv):
            out_v = out.rearrange("(n g) (h p) d -> n p g h d", g=PAIR, p=P)
            actv.wait_ge(sem["const_loaded"], 16 * N_CONST)
            for l in range(2):
                actv.activation(decay[l], decay[l], ACT.Exp).then_inc(sem["decay_exp"], 1)
            with actv.Fori(0, TURNS) as turn:
                order = [0]

                def in_order(ins):
                    ins.then_inc(sem["act_order"], 1)
                    order[0] += 1
                    actv.wait_ge(sem["act_order"], order[0])

                def flip_out(t, dst, scale=None):
                    for k in range(KD):
                        actv.wait_ge(sem["flip_ps"], KD * t + k + 1)
                        if scale is None:
                            ins = actv.activation(dst[:, k, :], ps[:, 6 + k, :], ACT.Copy)
                        else:
                            ins = actv.activation(dst[:, k, :], ps[:, 6 + k, :], ACT.Copy, scale=scale[:, k:k + 1])
                        ins.then_inc(sem["flip_sb"], 1)

                def attention(n):
                    for k in range(KD):
                        actv.wait_ge(sem["qkv_ps"], 6 * n + k + 1)
                        if n == 0:
                            ins = actv.activation(qT[:, k, :], ps[:, k, :], ACT.Copy, scale=DH ** -0.5)
                        else:
                            ins = actv.activation(qT[:, k, :], ps[:, k, :], ACT.Identity,
                                                  scale=DH ** -0.5, bias=b_qk[n][:, 0, k:k + 1])
                        ins.then_inc(sem["q_sb"], 1)
                    for k in range(KD):
                        actv.wait_ge(sem["qkv_ps"], 6 * n + 2 + k + 1)
                        if n == 0:
                            ins = actv.activation(k_all[:, k, :], ps[:, 2 + k, :], ACT.Copy)
                        else:
                            ins = actv.activation(k_all[:, k, :], ps[:, 2 + k, :], ACT.Identity,
                                                  bias=b_qk[n][:, 1, k:k + 1])
                        ins.then_inc(sem["k_sb"], 1)
                    for k in range(2):
                        actv.wait_ge(sem["qkv_ps"], 6 * n + 4 + k + 1)
                        for i in range(2):
                            actv.activation(
                                v_sb[i][:, 2 * k:2 * k + 2, :].rearrange("p t (h o d) -> p (t h) o d", o=2, d=DH)[:, :, i],
                                ps[:, 4 + k, :].rearrange("p (h o d) -> p h o d", o=2, d=DH)[:, :, i],
                                ACT.Copy).then_inc(sem["v_sb"], 1)

                    def evacuate(g):
                        actv.wait_ge(sem["probsT_ps"], GROUPS * n + g + 1)
                        if g >= 2:
                            actv.wait_ge(sem["pv_done"], GROUPS * n + g - 1)
                        actv.activation(probsT[g % 2], ps[:, 4:6, :], ACT.Copy).then_inc(sem["probsT_sb"], 1)

                    for g in range(GROUPS):
                        tt, c = g // QUADS, g % QUADS
                        w = attn_shape(n, tt) * P
                        actv.wait_ge(sem["max_ready"], GROUPS * n + g + 1)
                        if g >= 2:
                            actv.wait_ge(sem["probsT_ps"], GROUPS * n + g - 1)
                        for i in range(4):
                            if n == 2:
                                src = scaled[g % 3][:, i, :]
                            else:
                                src = ps[:, 2 * (g % 2) + i // 2, 256 * (i % 2):256 * (i % 2) + w]
                            h = 4 * c + i
                            ins = actv.activation(probs[g % 2][:, i, 0:w], src, ACT.Exp,
                                                  bias=neg_max[:, tt, h:h + 1],
                                                  accum_out=row_sum[:, tt, h:h + 1])
                        ins.then_inc(sem["probs_ready"], 1)
                        if n == 2 and g >= 1:
                            evacuate(g - 1)
                    if n == 2:
                        evacuate(GROUPS - 1)
                    actv.wait_ge(sem["pv_done"], GROUPS * (n + 1))
                    actv.activation(oT_sb, ps[:, 6:8, :], ACT.Copy).then_inc(sem["oT_ready"], 1)

                def ffn():
                    actv.wait_ge(sem["q8T_ps"], 1)
                    actv.activation(q8T.rearrange("p k t -> p (k t)"), ps[:, 6, :].bitcast(BF16),
                                    ACT.Copy).then_inc(sem["q8T_sb"], 1)
                    actv.wait_ge(sem["back_ps"], 1)
                    actv.activation(back_rows, ps[:, 7, :], ACT.Copy, scale=unquant[:, 0:1])\
                        .then_inc(sem["back_sb"], 1)
                    for m in range(MH + 1):
                        if m < MH:
                            actv.wait_ge(sem["up_sb"], m + 1)
                            actv.activation(act[:, m, :], up[m % 2], ACT.Identity, scale=conv3_w[:, m, 1:2],
                                            bias=conv3_b[:, m:m + 1]).then_inc(sem["conv_mid"], 1)
                        if m >= 1:
                            actv.wait_ge(sem["conv3_done"], m)
                            actv.activation(act[:, m - 1, :], act[:, m - 1, :], ACT.Silu)\
                                .then_inc(sem["act_ready"], 1)
                    for t in range(TT + 1):
                        if t < TT:
                            actv.wait_ge(sem["scale2_ready"], t + 1)
                            actv.activation(rounded[t % 2], ps[:, 2 * (t % 2):2 * (t % 2) + 2, :].rearrange("p a b -> p (a b)"),
                                            ACT.Identity, scale=q_scale[:, t:t + 1], bias=magic[:, 0:1])\
                                .then_inc(sem["rounded_ready"], 1)
                        if t >= 1:
                            actv.wait_ge(sem["q8hT_ps"], t)
                            actv.activation(q8hT[(t - 1) % 2].rearrange("p m t -> p (m t)"),
                                            ps[:, 4 + (t - 1) % 2, :].bitcast(BF16), ACT.Copy)\
                                .then_inc(sem["q8hT_sb"], 1)

                def mamba(l):
                    flip_out(5 + l, xT, norm_w[l])
                    for m in range(2 * DT):
                        actv.wait_ge(sem["in_ps"], 8 * l + m + 1)
                        if m < DT:
                            ins = actv.activation(xp[:, m, :], ps[:, m % 4, :], ACT.Identity, bias=b_in[l][:, m:m + 1])
                        else:
                            ins = actv.activation(gate_res[:, m - DT, :], ps[:, m % 4, :], ACT.Silu,
                                                  bias=b_in[l][:, m:m + 1])
                        ins.then_inc(sem["in_sb"], 1)
                    for m in range(DT):
                        actv.wait_ge(sem["conv5_done"], DT * l + m + 1)
                        actv.activation(xs[:, m, :], xs[:, m, :], ACT.Silu).then_inc(sem["xs_ready"], 1)
                    actv.wait_ge(sem["xdbl_ps"], 2 * l + 1)
                    actv.activation(low_rank[0:DTR, :], ps[0:DTR, 4, :], ACT.Copy).then_inc(sem["low_rank_sb"], 1)
                    actv.wait_ge(sem["xdbl_ps"], 2 * l + 2)
                    actv.activation(bc_rest[0:BC3, :], ps[0:BC3, 5, :], ACT.Copy).then_inc(sem["bc_sb"], 1)
                    for m in range(DT):
                        actv.wait_ge(sem["dt_ps"], DT * l + m + 1)
                        actv.activation(xp[:, m, :], ps[:, m, :], ACT.Abs, bias=b_dt[l][:, m:m + 1])
                        ins = actv.activation(delta[:, m, :], ps[:, m, :], ACT.Relu, bias=b_dt[l][:, m:m + 1])
                    in_order(ins)
                    flat = xp.rearrange("p m t -> p (m t)")
                    in_order(actv.activation(flat, flat, ACT.Exp, scale=-1.0))
                    actv.activation(flat, flat, ACT.Ln, bias=ones[:, 0:1]).then_inc(sem["ln_ready"], 1)
                    bc_out(l, 0)
                    actv.wait_ge(sem["delta_ready"], l + 1)
                    for s in range(STEPS):
                        c, m = s // DT, s % DT
                        if s >= 2:
                            actv.wait_ge(sem["h_ready"], l * STEPS + s - 1)
                        for i in range(NC):
                            n = c * NC + i
                            ins = actv.activation(dA[s % 2][:, i, :].rearrange("p (g t) -> p g t", g=PAIR)[:, :, 1:],
                                                  delta[:, m, :].rearrange("p (g t) -> p g t", g=PAIR)[:, :, 1:],
                                                  ACT.Exp, scale=decay[l][:, m, n:n + 1])
                        ins.then_inc(sem["dA_ready"], 1)
                        if m == 2 and c + 1 < CHUNKS:
                            bc_out(l, c + 1)

                def bc_out(l, c):
                    actv.wait_ge(sem["bc_ps"], l * CHUNKS + c + 1)
                    if c >= 2:
                        actv.wait_ge(sem["hc_ready"], l * STEPS + DT * (c - 1))
                    actv.activation(b_bc[c % 2], ps[:, 4:6, :], ACT.Copy).then_inc(sem["b_bc_ready"], 1)
                    actv.activation(c_bc[c % 2], ps[:, 6:8, :], ACT.Copy).then_inc(sem["c_bc_ready"], 1)

                def moe():
                    flip_out(9, xT)
                    for k in range(KD):
                        actv.wait_ge(sem["t_ps"], k + 1)
                        actv.activation(tT[:, k, :], ps[:, k, :], ACT.Identity, bias=b_m[:, k:k + 1])\
                            .then_inc(sem["t_sb"], 1)
                    actv.wait_ge(sem["t_sb"], KD)
                    actv.wait_ge(sem["t_zeroed"], 4)
                    for j in range(4):
                        rows = slice(32 * j, 32 * j + 32)
                        actv.activation(tT_head[j][rows], tT[rows], ACT.Copy).then_inc(sem["t_head_sb"], 1)
                    actv.wait_ge(sem["logits_ready"], 1)
                    actv.activation(pr, lg, ACT.Exp).then_inc(sem["router_exp"], 1)
                    actv.wait_ge(sem["gatesT_ps"], 1)
                    actv.activation(gatesT, ps[:, 6, :], ACT.Copy).then_inc(sem["gatesT_sb"], 1)
                    for k in range(KD):
                        actv.wait_ge(sem["b2_ps"], k + 1)
                        actv.activation(acc[:, k, :], ps[:, 4 + k, :], ACT.Copy).then_inc(sem["acc_set"], 1)
                    for w in range(EXP * KD * 2):
                        v, e = w // 2, w // 4
                        actv.wait_ge(sem["up_e_ps"], w + 1)
                        if w % 2 == 0 and v >= 2:
                            actv.wait_ge(sem["down_e_done"], v - 1)
                        actv.activation(hmid[v % 2][:, 2 * (w % 2):2 * (w % 2) + 2, :],
                                        ps[:, 2 * (w % 2):2 * (w % 2) + 2, :], ACT.Gelu,
                                        bias=b_e1[:, e:e + 1]).then_inc(sem["hmid_ready"], 1)

                flip_out(0, ctxT)
                flip_out(1, xT)
                attention(0)
                flip_out(3, xT)
                attention(1)
                ffn()
                mamba(0)
                mamba(1)
                flip_out(7, xT)
                attention(2)
                moe()
                actv.wait_ge(sem["x_done"], 1)
                for g in range(PAIR):
                    actv.dma_start(out_v[turn, :, g], halves(x)[:, g]).then_inc(sem["stored"], 16)
                end_turn(actv, turn)
            actv.wait_ge(sem["stored"], TURNS * PAIR * 16 + 1)

        @block.vector
        def _(dve):
            setup = [0]

            def in_setup_order(ins):
                ins.then_inc(sem["dve_setup"], 1)
                setup[0] += 1
                dve.wait_ge(sem["dve_setup"], setup[0])

            dve.memset(magic[:], ROUND)
            in_setup_order(dve.memset(ones[:], 1.0))
            dve.wait_ge(sem["const_loaded"], 16 * N_CONST)
            for i in range(3):
                rows = slice(2 * NS * i, 2 * NS * (i + 1))
                dve.tensor_copy(same_of_three[rows, :], ident[rows, rows])
            for exact, src in [(ident_bf, ident[:]), (causal_bf, causal_f), (window_bf, window_f),
                               (gate_sel, gate_sel_f)]:
                dve.tensor_copy(exact[:], src)
            dve.wait_ge(sem["ternary_loaded"], 16 * 2)
            flat_w = [w_up_f.rearrange("p a b -> p (a b)"), w_down_f.rearrange("p a b -> p (a b)")]
            flat_q = [w_up[:].rearrange("p a b -> p (a b)"), w_down[:].rearrange("p a b -> p (a b)")]
            for i in range(2):
                ins = dve.tensor_reduce(w_sum[:, i:i + 1], flat_w[i], AX.X, ALU.add, apply_absolute_value=True)
            ins.then_inc(sem["w_sum_ready"], 1)
            dve.wait_ge(sem["w_sum_ps"], 1)
            in_setup_order(dve.tensor_scalar(unquant[:], ps[:, 0, 0:2], 1.0 / (D * HID), 1e-5, ALU.mult, ALU.max))
            in_setup_order(dve.reciprocal(w_scale, unquant[:]))
            for i in range(2):
                dve.tensor_scalar(flat_w[i], flat_w[i], w_scale[:, i:i + 1], ROUND, ALU.mult, ALU.add)\
                    .then_inc(sem["dve_setup"], 1)
                setup[0] += 1
            dve.wait_ge(sem["dve_setup"], setup[0])
            for i in range(2):
                dve.tensor_scalar(flat_w[i], flat_w[i], ROUND, 1.0, ALU.subtract, ALU.min)\
                    .then_inc(sem["dve_setup"], 1)
                setup[0] += 1
            dve.wait_ge(sem["dve_setup"], setup[0])
            for i in range(2):
                in_setup_order(dve.tensor_scalar(flat_q[i], flat_w[i], -1.0, None, ALU.max))
            dve.nop().then_inc(sem["ternary_ready"], 1)
            dve.wait_ge(sem["decay_exp"], 2)
            for l in range(2):
                in_setup_order(dve.tensor_scalar(decay[l], decay[l], -1.0, None, ALU.mult))
            dve.wait_ge(sem["attn_w_loaded"], 16 * N_ATTN)
            for n in (1, 2):
                ins = dve.tensor_scalar(b_qk[n][:, 0, :], b_qk[n][:, 0, :], DH ** -0.5, None, ALU.mult)
            in_setup_order(ins)
            dve.nop().then_inc(sem["setup_done"], 1)

            with dve.Fori(0, TURNS) as turn:
                order = [0]

                def mark(ins):
                    ins.then_inc(sem["dve_order"], 1)
                    order[0] += 1

                def in_order(ins=None):
                    if ins is not None:
                        mark(ins)
                    dve.wait_ge(sem["dve_order"], order[0])

                def norm(u, src, rms=False, dst=None):
                    dst = xn if dst is None else dst
                    for t in range(TT):
                        ins = dve.bn_stats(stats[:, t, :], src[:, t, :])
                    in_order(ins)
                    for t in range(TT):
                        ins = dve.bn_aggr(mean_var[:, t, :], stats[:, t, :])
                    in_order(ins)
                    mean, var = mean_var[:, :, 0], mean_var[:, :, 1]
                    if rms:
                        in_order(dve.tensor_tensor(sq[:], mean, mean, ALU.mult))
                        ins = dve.scalar_tensor_tensor(out=var_eps[:], in0=var, scalar=EPS, in1=sq[:],
                                                       op0=ALU.add, op1=ALU.add)
                    else:
                        ins = dve.tensor_scalar(var_eps[:], var, EPS, None, ALU.add)
                    ins.then_inc(sem["var_ready"], 1)
                    dve.wait_ge(sem["rstd_ready"], u + 1)
                    for t in range(TT):
                        if rms:
                            ins = dve.tensor_scalar(dst[:, t, :], src[:, t, :], rstd[:, t:t + 1], None, ALU.mult)
                        else:
                            ins = dve.tensor_scalar(dst[:, t, :], src[:, t, :], mean_var[:, t, 0:1],
                                                    rstd[:, t:t + 1], ALU.subtract, ALU.mult)
                        ins.then_inc(sem["xn_ready"], 1)

                def residual(r, src, dst, last=None):
                    for p in range(2):
                        dve.wait_ge(sem["res_ps"], 2 * r + p + 1)
                        mark(dve.tensor_tensor(dst[:, 2 * p:2 * p + 2, :], src[:, 2 * p:2 * p + 2, :],
                                               ps[:, p, :].rearrange("p (t d) -> p t d", t=2), ALU.add))
                    in_order()

                def attention(n):
                    for g in range(POOL_QUAD):
                        dve.wait_ge(sem["k_sb"], KD * n + g // 2 + 1)
                        for i in range(4):
                            j, m = 4 * (g % 2) + i, g // 2
                            ins = dve.tensor_scalar(kT[j][:, m, :], k_all[:, m, :], head_rows[:, j:j + 1], None, ALU.mult)
                        ins.then_inc(sem["k_masked"], 1)

                    def maxima(g):
                        tt, c = g // QUADS, g % QUADS
                        w = attn_shape(n, tt) * P
                        if n == 2:
                            dve.wait_ge(sem["masked_ready"], g + 1)
                            src = scaled[g % 3]
                        else:
                            dve.wait_ge(sem["scores_ps"], GROUPS * n + g + 1)
                            src = ps[:, 2 * (g % 2):2 * (g % 2) + 2, :].rearrange("p a (b c) -> p (a b) c", b=2)[:, :, 0:w]
                        dve.tensor_reduce(neg_max[:, tt, 4 * c:4 * c + 4], src, AX.X, ALU.max, negate=True)\
                            .then_inc(sem["max_ready"], 1)

                    def scale(g):
                        dve.wait_ge(sem["scores_ps"], GROUPS * n + g + 1)
                        if g >= 3:
                            dve.wait_ge(sem["probs_ready"], GROUPS * n + g - 2)
                        rows = side[:, g // QUADS:g // QUADS + 1, :].to_broadcast([P, 4, S])
                        src = ps[:, 2 * (g % 2):2 * (g % 2) + 2, :].rearrange("p a (b c) -> p (a b) c", b=2)
                        dve.tensor_tensor(scaled[g % 3], src, rows, ALU.mult).then_inc(sem["scaled_ready"], 1)

                    def evacuate(g):
                        dve.wait_ge(sem["probsT_ps"], GROUPS * n + g + 1)
                        if g >= 2:
                            dve.wait_ge(sem["pv_done"], GROUPS * n + g - 1)
                        w = attn_shape(n, g // QUADS)
                        dve.tensor_copy(probsT[g % 2][:, 0:w, :], ps[:, 4:4 + w, :]).then_inc(sem["probsT_sb"], 1)

                    def inverse(tt):
                        dve.wait_ge(sem["probs_ready"], GROUPS * n + QUADS * (tt + 1))
                        in_order(dve.reciprocal(row_rec[:, tt, :], row_sum[:, tt, :]))
                        dve.tensor_copy(xn[:, tt, :].rearrange("p (h d) -> p h d", d=DH),
                                        row_rec[:, tt, :].unsqueeze(2).to_broadcast([P, HEADS, DH]))\
                            .then_inc(sem["inverse_ready"], 1)

                    for g in range(GROUPS + 1):
                        if n == 2:
                            if g < GROUPS:
                                scale(g)
                            if g >= 1:
                                maxima(g - 1)
                        else:
                            if g < GROUPS:
                                maxima(g)
                            if g >= 1:
                                evacuate(g - 1)
                        if g % QUADS == 2 and g > QUADS:
                            inverse(g // QUADS - 1)
                    inverse(TT - 1)
                    for k in range(KD):
                        dve.wait_ge(sem["oT_ready"], n + 1)
                        dve.wait_ge(sem["flip_ps"], KD * [2, 4, 8][n] + k + 1)
                        dve.tensor_tensor(xT[:, k, :], oT_sb[:, k, :], ps[:, k, :], ALU.mult).then_inc(sem["flip_sb"], 1)

                def ffn():
                    norm(2, x)
                    dve.wait_ge(sem["xn_ready"], 4 * 3)
                    in_order(dve.tensor_reduce(absmax, xn[:], AX.X, ALU.max, apply_absolute_value=True))
                    in_order(dve.tensor_scalar(absmax, absmax, 1e-5, None, ALU.max))
                    in_order(dve.reciprocal(q_scale, absmax))
                    in_order(dve.tensor_scalar(q_scale, q_scale, 127.0, None, ALU.mult))
                    in_order(dve.reciprocal(q_back, q_scale))
                    for t in range(TT):
                        dve.tensor_scalar(diag[:, t, :], ident[:], q_back[:, t:t + 1], None, ALU.mult)\
                            .then_inc(sem["diag_ready"], 1)
                    for t in range(TT):
                        mark(dve.tensor_scalar(xn[:, t, :], xn[:, t, :], q_scale[:, t:t + 1], ROUND, ALU.mult, ALU.add))
                    in_order()
                    in_order(dve.tensor_scalar(xn[:], xn[:], ROUND, -128.0, ALU.subtract, ALU.max))
                    dve.tensor_scalar(q8, xn[:], 127.0, None, ALU.min).then_inc(sem["q8_ready"], 1)
                    dve.wait_ge(sem["back_sb"], 1)

                    def rows(t):
                        return t.rearrange("p (g s) -> p g s", g=PAIR)

                    for m in range(MH + 1):
                        if m < MH:
                            dve.wait_ge(sem["up_ps"], m + 1)
                            if m >= 2:
                                dve.wait_ge(sem["conv3_done"], m - 1)
                            dve.tensor_tensor(up[m % 2], ps[:, m % 4, :], back_rows, ALU.mult)\
                                .then_inc(sem["up_sb"], 1)
                        if m >= 1:
                            j = m - 1
                            dve.wait_ge(sem["conv_mid"], m)
                            dve.wait_ge(sem["up_sb"], m)
                            o, u = rows(act[:, j, :]), rows(up[j % 2])
                            in_order(dve.scalar_tensor_tensor(out=o[:, :, 1:], in0=u[:, :, :-1], scalar=conv3_w[:, j, 0:1],
                                                              in1=o[:, :, 1:], op0=ALU.mult, op1=ALU.add))
                            dve.scalar_tensor_tensor(out=o[:, :, :-1], in0=u[:, :, 1:], scalar=conv3_w[:, j, 2:3],
                                                     in1=o[:, :, :-1], op0=ALU.mult, op1=ALU.add)\
                                .then_inc(sem["conv3_done"], 1)

                    for t in range(TT + 2):
                        if t < TT:
                            dve.wait_ge(sem["actT_ps"], t + 1)
                            src = ps[:, 2 * (t % 2):2 * (t % 2) + 2, :].rearrange("p a b -> p (a b)")
                            one = slice(t, t + 1)
                            in_order(dve.tensor_reduce(absmax[:, one], src, AX.X, ALU.max, apply_absolute_value=True))
                            in_order(dve.tensor_scalar(absmax[:, one], absmax[:, one], 1e-5, None, ALU.max))
                            in_order(dve.reciprocal(q_scale[:, one], absmax[:, one]))
                            dve.tensor_scalar(q_scale[:, one], q_scale[:, one], 127.0, None, ALU.mult)\
                                .then_inc(sem["scale2_ready"], 1)
                            dve.wait_ge(sem["scale2_ready"], t + 1)
                            in_order(dve.reciprocal(q_back[:, one], q_scale[:, one]))
                            in_order(dve.tensor_scalar(q_back[:, one], q_back[:, one], unquant[:, 1:2], None, ALU.mult))
                        if 1 <= t <= TT:
                            j = t - 1
                            dve.wait_ge(sem["rounded_ready"], t)
                            if j >= 2:
                                dve.wait_ge(sem["q8hT_ps"], j - 1)
                            in_order(dve.tensor_scalar(rounded[j % 2], rounded[j % 2], ROUND, -128.0, ALU.subtract, ALU.max))
                            dve.tensor_scalar(q8h[j % 2], rounded[j % 2], 127.0, None, ALU.min)\
                                .then_inc(sem["q8h_ready"], 1)
                        if t >= 2:
                            j = t - 2
                            dve.wait_ge(sem["down_ps"], j + 1)
                            in_order(dve.scalar_tensor_tensor(out=x[:, j, :], in0=ps[:, 6 + j % 2, 0:D],
                                                              scalar=q_back[:, j:j + 1], in1=x[:, j, :],
                                                              op0=ALU.mult, op1=ALU.add))

                def mamba(l):
                    norm(4 + l, h_res, rms=True)

                    def rows(t):
                        return t.rearrange("p (g s) -> p g s", g=PAIR)

                    if l == 0:
                        for i in range(2):
                            dve.memset(dA[i].rearrange("p n (g t) -> p (n g) t", g=PAIR)[:, :, 0:1], 0.0)\
                                .then_inc(sem["dA_heads"], 1)
                    for m in range(DT):
                        dve.wait_ge(sem["in_sb"], 8 * l + m + 1)
                        in_order(dve.tensor_scalar(xs[:, m, :], xp[:, m, :], conv5_w[l][:, m, 2:3],
                                                   conv5_b[l][:, m:m + 1], ALU.mult, ALU.add))
                        o, u = rows(xs[:, m, :]), rows(xp[:, m, :])
                        for k, shift in [(0, -2), (1, -1), (3, 1), (4, 2)]:
                            if shift < 0:
                                dst, src = o[:, :, -shift:], u[:, :, :shift]
                            else:
                                dst, src = o[:, :, :-shift], u[:, :, shift:]
                            ins = dve.scalar_tensor_tensor(out=dst, in0=src, scalar=conv5_w[l][:, m, k:k + 1], in1=dst,
                                                           op0=ALU.mult, op1=ALU.add)
                            if k < 4:
                                in_order(ins)
                        ins.then_inc(sem["conv5_done"], 1)
                    dve.wait_ge(sem["bc_sb"], l + 1)
                    for i in range(2):
                        in_order(dve.tensor_copy(bc_round[0:BC3, :], bc_rest[0:BC3, :]))
                        ins = dve.scalar_tensor_tensor(out=(bc if i else bc_rest)[0:BC3, :], in0=bc_round[0:BC3, :],
                                                       scalar=minus_part[0:BC3, i:i + 1], in1=bc_rest[0:BC3, :],
                                                       op0=ALU.mult, op1=ALU.add)
                        if i == 0:
                            in_order(ins)
                    ins.then_inc(sem["bc_split"], 1)
                    dve.wait_ge(sem["ln_ready"], l + 1)
                    dve.tensor_tensor(delta, delta, xp, ALU.add).then_inc(sem["delta_ready"], 1)
                    dve.wait_ge(sem["delta_ready"], l + 1)
                    dve.wait_ge(sem["xs_ready"], DT * (l + 1))
                    in_order(dve.tensor_tensor(du, delta, xs, ALU.mult))

                    def inject(s):
                        c, m = s // DT, s % DT
                        if m == 0:
                            dve.wait_ge(sem["b_bc_ready"], l * CHUNKS + c + 1)
                        if s >= 3:
                            dve.wait_ge(sem["y_added"], l * STEPS + s - 2)
                        dve.tensor_tensor(hbuf[s % 3], du[:, m:m + 1, :].to_broadcast([P, NC, TOK]), b_bc[c % 2], ALU.mult)\
                            .then_inc(sem["injected"], 1)

                    inject(0)
                    for s in range(STEPS):
                        if s + 1 < STEPS:
                            inject(s + 1)
                        dve.wait_ge(sem["dA_ready"], l * STEPS + s + 1)
                        dve.wait_ge(sem["injected"], l * STEPS + s + 1)
                        if s == 0 and l == 0:
                            dve.wait_ge(sem["dA_heads"], 2)
                        flat = hbuf[s % 3].rearrange("p n t -> p (n t)")
                        dve.tensor_tensor_scan(flat, dA[s % 2].rearrange("p n t -> p (n t)"), flat, 0.0,
                                               ALU.mult, ALU.add).then_inc(sem["h_ready"], 1)
                    for m in range(DT):
                        dve.wait_ge(sem["y_added"], l * STEPS + STEPS - DT + m + 1)
                        in_order(dve.scalar_tensor_tensor(out=xp[:, m, :], in0=xs[:, m, :], scalar=skip[l][:, m:m + 1],
                                                          in1=ps[:, m, :], op0=ALU.mult, op1=ALU.add))
                        dve.tensor_tensor(xp[:, m, :], xp[:, m, :], gate_res[:, m, :], ALU.mult)\
                            .then_inc(sem["y_ready"], 1)
                    residual(2 + l, h_res, h_res)

                def moe():
                    norm(8, x)
                    groups = TT * MHD

                    def over(t):
                        return t.unsqueeze(2).to_broadcast([P, groups, EXP])

                    dve.wait_ge(sem["logits_ps"], 1)
                    logit = ps[:, 7, :].rearrange("p (g e) -> p g e", e=EXP)
                    in_order(dve.tensor_reduce(best, logit, AX.X, ALU.max))
                    dve.tensor_tensor(lg, logit, over(best), ALU.subtract).then_inc(sem["logits_ready"], 1)
                    dve.wait_ge(sem["router_exp"], 1)
                    in_order(dve.tensor_reduce(z_sum, pr, AX.X, ALU.add))
                    in_order(dve.reciprocal(z_sum, z_sum))
                    in_order(dve.tensor_tensor(pr, pr, over(z_sum), ALU.mult))
                    ranks = rank.unsqueeze(1).to_broadcast([P, groups, EXP])

                    def choose(values, chosen):
                        in_order(dve.tensor_reduce(best, values, AX.X, ALU.max))
                        in_order(dve.tensor_tensor(pick, values, over(best), ALU.is_equal))
                        in_order(dve.tensor_tensor(pick, pick, ranks, ALU.mult))
                        in_order(dve.tensor_reduce(best, pick, AX.X, ALU.max))
                        in_order(dve.tensor_tensor(chosen, pick, over(best), ALU.is_equal))

                    choose(pr, first)
                    flat = "p g e -> p (g e)"
                    in_order(dve.scalar_tensor_tensor(out=left.rearrange(flat), in0=first.rearrange(flat), scalar=-2.0,
                                                      in1=pr.rearrange(flat), op0=ALU.mult, op1=ALU.add))
                    choose(left, lg)
                    in_order(dve.tensor_tensor(first, first, lg, ALU.add))
                    split = "p (t h) e -> p t h e"
                    dve.tensor_tensor(gates.rearrange("p t (e h) -> p t h e", e=EXP), pr.rearrange(split, t=TT),
                                      first.rearrange(split, t=TT), ALU.mult).then_inc(sem["gates_ready"], 1)
                    dve.wait_ge(sem["gatesT_sb"], 1)
                    in_order(dve.tensor_copy(gates_part[0], gatesT))
                    in_order(dve.tensor_tensor(gates_rest, gatesT, gates_part[0], ALU.subtract))
                    in_order(dve.tensor_copy(gates_part[1], gates_rest))
                    dve.tensor_tensor(gates_part[2], gates_rest, gates_part[1], ALU.subtract)\
                        .then_inc(sem["gates_split"], 1)
                    for v in range(EXP * KD):
                        dve.wait_ge(sem["gate_ps"], v + 1)
                        dve.tensor_copy(gate_bc[v % 2], ps[:, 6 + v % 2, :]).then_inc(sem["gate_sb"], 1)
                        dve.wait_ge(sem["down_e_done"], v + 1)
                        dve.wait_ge(sem["gate_sb"], v + 1)
                        if v >= 2:
                            dve.wait_ge(sem["acc_added"], v - 1)
                        dve.tensor_tensor(prod[v % 2], ps[:, 4 + v % 2, :], gate_bc[v % 2], ALU.mult)\
                            .then_inc(sem["prod_ready"], 1)
                    residual(5, x, x)

                dve.wait_ge(sem["x_loaded"], PAIR * 16 * (turn + 1))
                norm(0, x_in)
                attention(0)
                dve.wait_ge(sem["stored"], PAIR * 16 * turn + 1)
                residual(0, x_in, x)
                dve.nop().then_inc(sem["x_in_used"], 1)
                norm(1, x)
                attention(1)
                residual(1, x, x)
                ffn()
                norm(3, x, dst=h_res)
                dve.wait_ge(sem["xn_ready"], 4 * 4)
                mamba(0)
                mamba(1)
                norm(6, h_res, rms=True)
                dve.wait_ge(sem["xn_ready"], 4 * 7)
                in_order(dve.tensor_tensor(xn[:], xn[:], norm_f[:].unsqueeze(1).to_broadcast([P, TT, D]), ALU.mult))
                in_order(dve.tensor_tensor(x[:], x[:], xn[:], ALU.add))
                dve.wait_ge(sem["side_loaded"], 2 * PAIR * 16 * (turn + 1))
                in_order(dve.tensor_scalar(mask_in[:].bitcast(F32), mask_in[:], 0, -1e30, ALU.is_equal, ALU.mult))
                norm(7, x)
                attention(2)
                residual(4, x, x)
                dve.nop().then_inc(sem["side_used"], 1)
                moe()
                dve.nop().then_inc(sem["x_done"], 1)
                end_turn(dve, turn)

        @block.tensor
        def _(pe):
            pe.wait_ge(sem["const_loaded"], 16 * N_CONST)
            pe.wait_ge(sem["dve_setup"], 1)
            pe.wait_ge(sem["w_sum_ready"], 1)
            pe.matmul(ps[:, 0, 0:2], ones[:], w_sum, start=True, stop=True).then_inc(sem["w_sum_ps"], 1)
            pe.wait_ge(sem["setup_done"], 1)
            pe.wait_ge(sem["ternary_ready"], 1)

            with pe.Fori(0, TURNS) as turn:
                def flip(t, src, name, first_count, bank=6):
                    for tt in range(TT):
                        pe.wait_ge(sem[name], first_count + tt)
                        for k in range(KD):
                            ins = pe.transpose(ps[:, bank + k, of(0, tt)], src[:, tt, k * P:(k + 1) * P], ident[:])
                            if tt == TT - 1:
                                ins.then_inc(sem["flip_ps"], 1)

                def project_tokens(r, src, w, bias, tiles):
                    for tt in range(TT):
                        dst = ps[:, tt // 2, (tt % 2) * D:(tt % 2 + 1) * D]
                        if bias is not None:
                            b0 = 32 * (bias % 4)
                            pe.matmul(dst, ones[b0:b0 + 1, :], bias_rows[b0:b0 + 1, bias // 4, :], start=True, stop=False)
                        for k in range(tiles):
                            ins = pe.matmul(dst, src[:, k, of(0, tt)], w[:, k, :],
                                            start=(k == 0 and bias is None), stop=(k == tiles - 1))
                        if tt % 2:
                            ins.then_inc(sem["res_ps"], 1)

                def attention(n):
                    pe.wait_ge(sem["flip_sb"], 2 * [1, 3, 7][n] + 2)
                    w = {c: (w_qkv[:, :, i * D:(i + 1) * D] if n == 0 else w_attn[n, c][:])
                         for i, c in enumerate("qkv")}
                    kv = xT if n == 0 else ctxT
                    for i, (c, src) in enumerate([("q", xT), ("k", kv)]):
                        for m in range(KD):
                            for k in range(KD):
                                ins = pe.matmul(ps[:, 2 * i + m, :], w[c][:, k, m * P:(m + 1) * P], src[:, k, :],
                                                start=(k == 0), stop=(k == KD - 1))
                            ins.then_inc(sem["qkv_ps"], 1)
                    for tt in range(TT):
                        dst = ps[:, 4 + tt // 2, (tt % 2) * D:(tt % 2 + 1) * D]
                        if n > 0:
                            i = 2 * (n - 1)
                            b0 = 32 * (i % 4)
                            pe.matmul(dst, ones[b0:b0 + 1, :], bias_rows[b0:b0 + 1, i // 4, :], start=True, stop=False)
                        for k in range(KD):
                            ins = pe.matmul(dst, kv[:, k, of(0, tt)], w["v"][:, k, :],
                                            start=(k == 0 and n == 0), stop=(k == KD - 1))
                        if tt % 2:
                            ins.then_inc(sem["qkv_ps"], 1)

                    def scores(g):
                        tt, c = g // QUADS, g % QUADS
                        b = tt // 2
                        w_ = attn_shape(n, tt) * P
                        if g >= 2:
                            if n == 2:
                                pe.wait_ge(sem["scaled_ready"], g - 1)
                            else:
                                pe.wait_ge(sem["probs_ready"], GROUPS * n + g - 1)
                        if g < POOL_QUAD:
                            pe.wait_ge(sem["k_masked"], POOL_QUAD * n + g + 1)
                        elif g == POOL_QUAD:
                            pe.wait_ge(sem["k_masked_pool"], n + 1)
                        masked = n == 0 or (n == 1 and tt % 2 == 0)
                        for i in range(4):
                            h = 4 * c + i
                            m, j = h // 8, h % 8
                            dst = ps[:, 2 * (g % 2) + i // 2, 256 * (i % 2):256 * (i % 2) + w_]
                            ins = pe.matmul(dst, qT[:, m, of(0, tt)], kT[j][:, m, b * S:b * S + w_],
                                            start=True, stop=not masked)
                            if masked and n == 0:
                                ins = pe.matmul(dst[:, w_ - P:w_], ident_bf[:], causal_bf[:], start=False, stop=True)
                            elif masked:
                                ins = pe.matmul(dst, ident_bf[:], window_bf[:], start=False, stop=True)
                        ins.then_inc(sem["scores_ps"], 1)

                    def turn_probs(g):
                        pe.wait_ge(sem["probs_ready"], GROUPS * n + g + 1)
                        if g >= 1:
                            pe.wait_ge(sem["probsT_sb"], GROUPS * n + g)
                        for kt in range(attn_shape(n, g // QUADS)):
                            for i in range(4):
                                ins = pe.transpose(ps[:, 4 + kt, i * P:(i + 1) * P],
                                                   probs[g % 2][:, i, kt * P:(kt + 1) * P], ident[:])
                        ins.then_inc(sem["probsT_ps"], 1)

                    def values(g):
                        tt, c = g // QUADS, g % QUADS
                        pe.wait_ge(sem["probsT_sb"], GROUPS * n + g + 1)
                        kts = attn_shape(n, tt)
                        for kt in range(kts):
                            for odd in range(2):
                                for pair in range(2):
                                    i = 2 * pair + odd
                                    col = 32 * ((2 * c + pair) % 4)
                                    lo = 4 * c * DH + 32 * pair
                                    ins = pe.matmul(ps[col:col + 32, 6 + c // 2, of(0, tt)],
                                                    v_sb[odd][:, 2 * (tt // 2) + kt, lo:lo + 32],
                                                    probsT[g % 2][:, kt, i * P:(i + 1) * P],
                                                    start=(kt == 0 and odd == 0), stop=(kt == kts - 1 and odd == 1))
                        ins.then_inc(sem["pv_done"], 1)

                    pe.wait_ge(sem["q_sb"], KD * (n + 1))
                    pe.wait_ge(sem["k_sb"], KD * (n + 1))
                    pe.wait_ge(sem["v_sb"], 4 * (n + 1))
                    pe.wait_ge(sem["v_zeroed"], 2 * (n + 1))
                    ahead = 3 if n == 2 else 1
                    for g in range(ahead):
                        scores(g)
                    for g in range(GROUPS):
                        if g + ahead < GROUPS:
                            scores(g + ahead)
                        turn_probs(g)
                        if g >= 1:
                            values(g - 1)
                    values(GROUPS - 1)
                    flip([2, 4, 8][n], xn, "inverse_ready", TT * n + 1, bank=0)
                    pe.wait_ge(sem["flip_sb"], 2 * [2, 4, 8][n] + 2)
                    project_tokens([0, 1, 4][n], xT, w_attn[n, "o"], None if n == 0 else 2 * n - 1, KD)

                def ffn():
                    pe.wait_ge(sem["q8_ready"], 1)
                    flat = ps[:, 6, :].bitcast(BF16)
                    for k in range(KD):
                        for tt in range(TT):
                            ins = pe.transpose(flat[:, k * TOK + tt * P:k * TOK + (tt + 1) * P],
                                               q8[:, tt, k * P:(k + 1) * P], ident_bf[:])
                    ins.then_inc(sem["q8T_ps"], 1)
                    pe.wait_ge(sem["diag_ready"], TT)
                    for tt in range(TT):
                        ins = pe.matmul(ps[:, 7, of(0, tt)], ones[:], diag[:, tt, :], start=True, stop=True)
                    ins.then_inc(sem["back_ps"], 1)
                    pe.wait_ge(sem["q8T_sb"], 1)
                    for m in range(MH):
                        if m >= 4:
                            pe.wait_ge(sem["up_sb"], m - 3)
                        for k in range(KD):
                            ins = pe.matmul(ps[:, m % 4, :], w_up[:, k, m * P:(m + 1) * P], q8T[:, k, :],
                                            start=(k == 0), stop=(k == KD - 1))
                        ins.then_inc(sem["up_ps"], 1)
                    pe.wait_ge(sem["act_ready"], MH)

                    def turn_act(tt):
                        if tt >= 2:
                            pe.wait_ge(sem["rounded_ready"], tt - 1)
                        for m in range(MH):
                            bank = 2 * (tt % 2) + m // 4
                            ins = pe.transpose(ps[:, bank, (m % 4) * P:(m % 4 + 1) * P], act[:, m, of(0, tt)], ident[:])
                        ins.then_inc(sem["actT_ps"], 1)

                    turn_act(0)
                    turn_act(1)
                    for tt in range(TT):
                        pe.wait_ge(sem["q8h_ready"], tt + 1)
                        if tt >= 2:
                            pe.wait_ge(sem["q8hT_sb"], tt - 1)
                        flat = ps[:, 4 + tt % 2, :].bitcast(BF16)
                        for m in range(MH):
                            ins = pe.transpose(flat[:, m * P:(m + 1) * P], q8h[tt % 2][:, m * P:(m + 1) * P], ident_bf[:])
                        ins.then_inc(sem["q8hT_ps"], 1)
                        if tt + 2 < TT:
                            turn_act(tt + 2)
                        pe.wait_ge(sem["q8hT_sb"], tt + 1)
                        for m in range(MH):
                            ins = pe.matmul(ps[:, 6 + tt % 2, 0:D], q8hT[tt % 2][:, m, :], w_down[:, m, :],
                                            start=(m == 0), stop=(m == MH - 1))
                        ins.then_inc(sem["down_ps"], 1)

                def mamba(l):
                    if l == 0:
                        pe.wait_ge(sem["rest_w_loaded"], 16 * N_REST)
                    flip(5 + l, xn, "xn_ready", 4 * (4 + l) + 1)
                    pe.wait_ge(sem["flip_sb"], 2 * (5 + l) + 2)
                    for m in range(2 * DT):
                        if m >= 4:
                            pe.wait_ge(sem["in_sb"], 8 * l + m - 3)
                        for k in range(KD):
                            ins = pe.matmul(ps[:, m % 4, :], w_in[l][:, k, m * P:(m + 1) * P], xT[:, k, :],
                                            start=(k == 0), stop=(k == KD - 1))
                        ins.then_inc(sem["in_ps"], 1)
                    for part_, (bank, lo, hi) in enumerate([(4, 0, DTR), (5, DTR, DTR + BC3)]):
                        for m in range(DT):
                            pe.wait_ge(sem["xs_ready"], DT * l + m + 1)
                            ins = pe.matmul(ps[0:hi - lo, bank, :], w_x[l][:, m, lo:hi], xs[:, m, :],
                                            start=(m == 0), stop=(m == DT - 1))
                        ins.then_inc(sem["xdbl_ps"], 1)
                    pe.wait_ge(sem["low_rank_sb"], l + 1)
                    for m in range(DT):
                        pe.matmul(ps[:, m, :], w_dt[l][:, m * P:(m + 1) * P], low_rank[0:DTR, :], start=True, stop=True)\
                            .then_inc(sem["dt_ps"], 1)
                    pe.wait_ge(sem["bc_split"], l + 1)

                    def spread(c):
                        if c >= 1:
                            pe.wait_ge(sem["c_bc_ready"], l * CHUNKS + c)
                        for i in range(NC):
                            for which in range(2):
                                r = which * NS + c * NC + i
                                ins = pe.matmul(ps[:, 4 + 2 * which + i, :],
                                                same_of_three[0:BC3, r:r + 1].to_broadcast([BC3, P]),
                                                bc[0:BC3, :], start=True, stop=True)
                        ins.then_inc(sem["bc_ps"], 1)

                    spread(0)
                    pe.wait_ge(sem["ln_ready"], l + 1)
                    for s in range(STEPS):
                        c, m = s // DT, s % DT
                        if m == 0 and c + 1 < CHUNKS:
                            spread(c + 1)
                        pe.wait_ge(sem["hc_ready"], l * STEPS + s + 1)
                        for i in range(NC):
                            ins = pe.matmul(ps[:, m, :], ident[:], hbuf[s % 3][:, i, :], start=(c == 0 and i == 0),
                                            stop=(c == CHUNKS - 1 and i == NC - 1))
                        ins.then_inc(sem["y_added"], 1)
                    pe.wait_ge(sem["y_ready"], DT * (l + 1))
                    project_tokens(2 + l, xp, w_out[l], 4 + l, DT)

                def moe():
                    flip(9, xn, "xn_ready", 4 * 8 + 1)
                    pe.wait_ge(sem["flip_sb"], 20)
                    for m in range(KD):
                        for k in range(KD):
                            ins = pe.matmul(ps[:, m, :], w_m[:, k, m * P:(m + 1) * P], xT[:, k, :],
                                            start=(k == 0), stop=(k == KD - 1))
                        ins.then_inc(sem["t_ps"], 1)
                    pe.wait_ge(sem["t_sb"], KD)
                    for tt in range(TT):
                        for k in range(KD):
                            at = (tt * KD + k) * 4 * EXP
                            ins = pe.matmul(ps[:, 7, at:at + 4 * EXP], tT[:, k, of(0, tt)], emb[:], start=True, stop=True)
                    ins.then_inc(sem["logits_ps"], 1)

                    def up_e(w):
                        e, k, half = w // 4, w // 2 % 2, w % 2
                        if w >= 2:
                            pe.wait_ge(sem["hmid_ready"], w - 1)
                        if w < 2:
                            pe.wait_ge(sem["t_head_sb"], 2 * w + 2)
                        for i in range(2):
                            ins = pe.matmul(ps[:, 2 * (w % 2) + i, :], w_e1[:, e, :], tT_head[2 * half + i][:, k, :],
                                            start=True, stop=True)
                        ins.then_inc(sem["up_e_ps"], 1)

                    up_e(0)
                    pe.wait_ge(sem["gates_ready"], 1)
                    for tt in range(TT):
                        ins = pe.transpose(ps[:, 6, of(0, tt)], gates[:, tt, :], ident[:])
                    ins.then_inc(sem["gatesT_ps"], 1)
                    pe.wait_ge(sem["gatesT_sb"], 1)
                    for k in range(KD):
                        pe.matmul(ps[:, 4 + k, :], b_e2[:, k, :], gatesT, start=True, stop=True).then_inc(sem["b2_ps"], 1)
                    up_e(1)

                    def spread_gate(v):
                        if v >= 2:
                            pe.wait_ge(sem["gate_sb"], v - 1)
                        for i in range(3):
                            ins = pe.matmul(ps[:, 6 + v % 2, :], gate_sel[:, v, :], gates_part[i], start=(i == 0),
                                            stop=(i == 2))
                        ins.then_inc(sem["gate_ps"], 1)

                    pe.wait_ge(sem["gates_split"], 1)
                    spread_gate(0)
                    for v in range(EXP * KD):
                        if v + 1 < EXP * KD:
                            up_e(2 * v + 2)
                            spread_gate(v + 1)
                            up_e(2 * v + 3)
                        pe.wait_ge(sem["hmid_ready"], 2 * v + 2)
                        if v >= 2:
                            pe.wait_ge(sem["prod_ready"], v - 1)
                        else:
                            pe.wait_ge(sem["acc_set"], v + 1)
                        for j in range(4):
                            ins = pe.matmul(ps[32 * j:32 * j + 32, 4 + v % 2, :], w_e2[:, v // KD, :],
                                            hmid[v % 2][:, j, :], start=True, stop=True)
                        ins.then_inc(sem["down_e_done"], 1)
                    pe.wait_ge(sem["acc_added"], EXP * KD)
                    project_tokens(5, acc, w_mo, 6, KD)

                pe.wait_ge(sem["ctx_loaded"], PAIR * 16 * (turn + 1))
                for tt in range(TT):
                    for k in range(KD):
                        ins = pe.transpose(ps[:, 6 + k, of(0, tt)], ctx_in[:, tt, k * P:(k + 1) * P], ident[:])
                        if tt == TT - 1:
                            ins.then_inc(sem["flip_ps"], 1)
                pe.wait_ge(sem["flip_sb"], 2)
                pe.nop().then_inc(sem["ctx_in_used"], 1)
                flip(1, xn, "xn_ready", 1)
                attention(0)
                flip(3, xn, "xn_ready", 5)
                attention(1)
                ffn()
                mamba(0)
                mamba(1)
                flip(7, xn, "xn_ready", 29)
                attention(2)
                moe()
                end_turn(pe, turn)


def layouts(inp):
    import numpy as np

    def arr(name):
        return np.asarray(inp[name])

    def T(w):
        return np.ascontiguousarray(w.T)

    a = {"x": arr("x"), "ctx": arr("ctx_1024"), "side": arr("fside_BxSxS2_0"),
         "mask": arr("mask_Bx1xSxS2_if1").reshape(B, S, S)}
    a["qkvT"], a["projT"] = T(arr("L0_attn_w_qkv")), T(arr("L0_attn_w_proj"))
    small = {}

    def by_partition(v):
        v = v.reshape(-1, P, *v.shape[1:])
        return np.moveaxis(v, 1, 0).reshape(P, -1)

    for n, pre in ((1, "L0_xattn_"), (2, "L1_xattn_")):
        for c in "qkvo":
            a[f"x{n}_{c}T"] = T(arr(f"{pre}W{c}"))
        small[f"b_qk{n}"] = np.concatenate([by_partition(arr(pre + "bq")), by_partition(arr(pre + "bk"))], 1)
        for c in "vo":
            a[f"{pre}b{c}"] = arr(f"{pre}b{c}").reshape(1, D)
    a["w1T"], a["w2T"] = T(arr("L0_ffn_w1")), T(arr("L0_ffn_w2"))
    small["conv3_w"] = by_partition(arr("L0_ffn_conv_w").reshape(HID, 3))
    small["conv3_b"] = by_partition(arr("L0_ffn_conv_b"))
    for l in range(2):
        m = "L1_attn_"
        a[f"inT{l}"], a[f"xT{l}"] = T(arr(m + "in_proj_w")[l]), T(arr(m + "x_proj_w")[l])
        a[f"xT{l}"] = np.concatenate([a[f"xT{l}"]] + 2 * [a[f"xT{l}"][:, DTR:]], 1)
        a[f"dtT{l}"], a[f"outT{l}"] = T(arr(m + "dt_proj_w")[l]), T(arr(m + "out_proj_w")[l])
        a[f"out_b{l}"] = arr(m + "out_proj_b")[l].reshape(1, D)
        small[f"conv5_w{l}"] = by_partition(arr(m + "conv_w")[l].reshape(DI, TAPS))
        for name, source in [("b_in", "in_proj_b"), ("conv5_b", "conv_b"), ("b_dt", "dt_proj_b"), ("decay", "A_log"),
                             ("skip", "D"), ("norm_w", "norm_w")]:
            small[f"{name}{l}"] = by_partition(arr(m + source)[l])
    a["norm_f"] = arr("L1_attn_norm_f_w")
    f = "L1_ffn_"
    a["Wm"], a["Wo"], a["W1"], a["W2"] = (arr(f + c) for c in ("Wm", "Wo", "W1", "W2"))
    a["L1_ffn_bo"] = arr(f + "bo").reshape(1, D)
    small["b_m"], small["b_e1"] = by_partition(arr(f + "bm")), arr(f + "b1").T
    emb = np.zeros((P, 4 * EXP), np.float32)
    b2 = np.zeros((KD, MHD * EXP, P), np.float32)
    for j in range(4):
        emb[32 * j:32 * j + 32, EXP * j:EXP * (j + 1)] = arr(f + "expert_emb")
        for k in range(KD):
            h = 4 * k + j
            b2[k, h::MHD, MD * j:MD * (j + 1)] = arr(f + "b2")
    a["emb"], a["b2_rows"] = emb, b2
    i, j = np.arange(P)[:, None], np.arange(S)[None, :]
    a["c_ident"] = np.eye(P, dtype=np.float32)
    a["c_causal"] = np.where(j[:, :P] > i, -1e30, 0.0).astype(np.float32)
    a["c_window"] = np.where(j // 4 > i, -1e30, 0.0).astype(np.float32)
    sel = np.zeros((P, EXP * KD, 4, MD), np.float32)
    for v in range(EXP * KD):
        for h in range(4):
            sel[4 * v + h, v, h] = 1
    a["c_gate_sel"] = sel.reshape(P, EXP * KD, P)
    small["head_rows"] = (np.arange(P)[:, None] // DH == np.arange(P // DH)).astype(np.float32)
    third = np.arange(P) // (2 * NS)
    small["minus_part"] = np.stack([np.where(third >= i, -1.0, 0.0) for i in (1, 2)], 1).astype(np.float32)
    small["rank"] = np.tile(np.arange(EXP, 0, -1, dtype=np.float32), (P, 1))
    a["small"] = np.concatenate([small[name] for name, _ in SMALL], 1)
    return {k: np.ascontiguousarray(v) for k, v in a.items()}


def kernel(**inputs):
    import concourse.bacc as bacc
    from concourse.bass_utils import run_bass_kernel_spmd as run

    arrays = layouts(inputs)
    nc = bacc.Bacc("TRN2", target_bir_lowering=False, num_devices=1)
    aps = {k: nc.dram_tensor(f"in_{k}", v.shape, mybir.dt.from_np(v.dtype), kind="ExternalInput").ap()
           for k, v in arrays.items()}
    out = nc.dram_tensor("out_0", (B, S, D), F32, kind="ExternalOutput").ap()
    program(nc, aps, out)
    r = run(nc, [{f"in_{k}": v for k, v in arrays.items()}], core_ids=[0])
    return r.results[0]["out_0"]
```

```python
from contextlib import ExitStack

import concourse.bass as bass
from concourse import mybir

ALU = mybir.AluOpType
ACT = mybir.ActivationFunctionType
F32 = mybir.dt.float32
BF16 = mybir.dt.bfloat16
I32 = mybir.dt.int32
AX = mybir.AxisListType

P = 128
B, S, D = 8, 256, 256
PAIR = 2
TURNS = B // PAIR
TOK = PAIR * S
TT = TOK // P
KD = D // P
HEADS, DH = 16, 16
QUADS = HEADS // 4
GROUPS = TT * QUADS
PAIRS = GROUPS // 2
POOL_QUAD = QUADS - 1
HID = 1024
MH = HID // P
DI, NS, DTR, TAPS = 512, 16, 64, 5
DT = DI // P
NC = 2
CHUNKS = NS // NC
STEPS = CHUNKS * DT
BC3 = 3 * 2 * NS
MHD, EXP, EH = 8, 16, 128
MD = D // MHD
UP_AHEAD = 4
T_PARTS = ((0, 1, 2, 0), (1, 0, 2, 1))
EARLY_Z = 2
EPS = 1e-5
ROUND = 12582912.0

SMALL = ([(f"b_qk{n}", (2, KD)) for n in (1, 2)] + [("conv3_w", (MH, 3)), ("conv3_b", (MH,))]
         + [(name + str(l), shape) for l in range(2)
            for name, shape in [("b_in", (2 * DT,)), ("conv5_w", (DT, TAPS)), ("conv5_b", (DT,)), ("b_dt", (DT,)),
                                ("decay", (DT, NS)), ("skip", (DT,)), ("norm_w", (KD,))]]
         + [("b_m", (KD,)), ("b_e1", (EXP,)), ("head_rows", (8,)), ("rank", (EXP,))])
BIAS_ROWS = ["L0_xattn_bv", "L0_xattn_bo", "L1_xattn_bv", "L1_xattn_bo", "out_b0", "out_b1", "L1_ffn_bo"]


LASTING = """
    const_loaded ternary_loaded first_w_loaded expert_w_loaded attn_w_loaded rest_w_loaded   (weights and
    constants are in SBUF)
    expert_high expert_rest expert_middle expert_copied expert_low expert_last expert_w_ready
    w_scale_ready w_scaled
    dve_setup half_set w_sum_ready w_sum_ps decay_exp ternary_ready setup_done   (steps before the loop)
    x_loaded ctx_loaded side_loaded mask_loaded   (a turn's rows are in SBUF)
    stored   (a turn's result is in DRAM)
    turn_opened   (the semaphores of the turn before have been cleared)
"""
IN_TURN = """
    x_in_used ctx_in_used mask_used   (a turn's rows have been read: the next may be loaded)
    x_done turn_ended
    act_order dve_order   (an engine waits for its own results)
    var_ready rstd_ready xn_ready   (normalisation)
    flip_ps flip_sb   (token-major to feature-major)
    q_ps k_ps v_ps q_sb k_sb k_masked k_masked_pool v_zeroed v_sb scores_ps scaled_ready masked_ready
    max_ready probs_ready probsT_ps probsT_sb pv_done
    inverse_ready oT_ready res_ps   (attention; res_ps: what is added to the residual rows)
    q8_ready q8T_ps q8T_sb diag_ready back_ps back_sb up_ps up_sb conv_mid conv3_done act_ready actT_ps
    scale2_ready rounded_ready q8h_ready q8hT_ps q8hT_sb down_ps   (convolution MLP)
    in_ps in_sb gate_ready late_z_sb conv5_mid last_tap_ready last_tap_added conv5_done xs_ready xdbl_ps
    low_rank_sb bc_sb bc_split dt_ps z_sb abs_ready ln_ready delta_ready bc_ps b_bc_ready
    c_bc_ready dA_heads dA_ready injected h_ready hc_ready y_added y_ready   (Mamba)
    t_ps t_sb t_high t_rest_ready t_split t_head_ps t_head_sb logits_ps logits_ready router_exp
    gates_ready gatesT_ps gatesT_sb gates_split block_ps block_sb b2_ps acc_set
    gate_ps gate_sb up_e_ps hmid_ready down_e_done prod_ready acc_added   (mixture of experts)
"""


def names_in(text):
    return " ".join(piece.split(")")[-1] for piece in text.split("(")).split()


def program(nc, a, out):
    with ExitStack() as ctx:
        def sb(name, shape, dt=F32):
            return ctx.enter_context(nc.sbuf_tensor(name, shape, dt))

        sem = {name: ctx.enter_context(nc.semaphore(name)) for name in names_in(IN_TURN) + names_in(LASTING)}
        in_turn = [sem[name].num for name in names_in(IN_TURN)]
        assert in_turn == list(range(in_turn[0], in_turn[0] + len(in_turn)))

        def end_turn(eng, turn):
            eng.nop().then_inc(sem["turn_ended"], 1)
            eng.wait_ge(sem["turn_opened"], turn + 1)

        ps = ctx.enter_context(nc.psum_tensor("ps", [P, 8, 512], F32))

        ident = sb("ident", [P, P])
        ident_bf = sb("ident_bf", [P, P], BF16)
        causal_bf = sb("causal_bf", [P, P], BF16)
        window_bf = sb("window_bf", [P, S], BF16)
        same_of_three = sb("same_of_three", [P, 2 * NS], BF16)
        ones = sb("ones", [P, P])
        magic = sb("magic", [P, 1])
        scratch = sb("scratch", [P, 1])
        minus_half = sb("minus_half", [P, TT])
        bias_rows = sb("bias_rows", [P, 2, D])

        def cells(shape):
            n = 1
            for s_ in shape:
                n *= s_
            return n

        small = sb("small", [P, sum(cells(shape) for _, shape in SMALL)])
        table, at_ = {}, 0
        for name_, shape in SMALL:
            ap = small[:, at_:at_ + cells(shape)]
            table[name_] = ap if len(shape) == 1 else ap.rearrange("p (a b) -> p a b", b=shape[1])
            at_ += cells(shape)
        b_qk = {n: table[f"b_qk{n}"] for n in (1, 2)}
        conv3_w, conv3_b = table["conv3_w"], table["conv3_b"]
        b_in, conv5_w, conv5_b, b_dt, decay, skip, norm_w = (
            [table[name_ + str(l)] for l in range(2)]
            for name_ in ("b_in", "conv5_w", "conv5_b", "b_dt", "decay", "skip", "norm_w"))
        b_m, b_e1 = table["b_m"], table["b_e1"]
        head_rows = table["head_rows"]
        rank = table["rank"]

        w_qkv = sb("w_qkv", [P, KD, 3 * D])
        w_attn = {(0, "o"): sb("w_proj", [P, KD, D])}
        for n in (1, 2):
            for c in "qkvo":
                w_attn[n, c] = sb(f"w_{c}{n}", [P, KD, D])
        w_up = sb("w_up", [P, KD, HID], BF16)
        w_down = sb("w_down", [P, MH, D], BF16)
        unquant = sb("unquant", [P, 2])
        w_in = [sb(f"w_in{l}", [P, KD, 2 * DI]) for l in range(2)]
        w_x = [sb(f"w_x{l}", [P, DT, DTR + 2 * NS]) for l in range(2)]
        w_dt = [sb(f"w_dt{l}", [DTR, DI]) for l in range(2)]
        w_out = [sb(f"w_out{l}", [P, DT, D]) for l in range(2)]
        norm_f = sb("norm_f", [P, D])
        w_m = sb("w_m", [P, KD, D])
        emb = sb("emb", [P, 4 * EXP])
        w_e1 = [sb(f"w_e1_{i}", [P, EXP, EH], BF16) for i in range(2)]
        w_e2 = sb("w_e2", [P, EXP, MD])
        b_e2 = sb("b_e2", [P, KD, P])
        w_mo = sb("w_mo", [P, KD, D])
        gate_sel = sb("gate_sel", [P, 8, P], BF16)

        x_in = sb("x_in", [P, TT, D])
        ctx_in = sb("ctx_in", [P, TT, D])
        side = sb("side", [P, TT, S])
        mask_in = sb("mask_in", [P, TT, S], I32)
        x = sb("x", [P, TT, D])
        xn = sb("xn", [P, TT, D])
        h_res = sb("h_res", [P, TT, D])
        xT = sb("xT", [P, KD, TOK])
        ctxT = sb("ctxT", [P, KD, TOK])
        stats = sb("stats", [P, TT, 6])
        mean_var = sb("mean_var", [P, TT, 2])
        sq = sb("sq", [P, TT])
        var_eps = sb("var_eps", [P, TT])
        rstd = sb("rstd", [P, TT])

        w_e1_f = [side[:].rearrange("p t (e i) -> p (t e) i", i=EH),
                  mask_in[:].bitcast(F32).rearrange("p t (e i) -> p (t e) i", i=EH)]

        REGION = 19648
        region = sb("region", [P, REGION])
        taken = [0]

        def part(shape, dt=F32):
            n = 1
            for s_ in shape:
                n *= s_
            words = n if dt != BF16 else n // 2
            at = taken[0]
            taken[0] += words
            assert taken[0] <= REGION, taken[0]
            ap = region[:, at:at + words]
            if dt == BF16:
                ap = ap.bitcast(BF16)
            names = "abcd"[:len(shape)]
            if len(shape) > 1:
                ap = ap.rearrange(f"p ({' '.join(names)}) -> p {' '.join(names)}",
                                  **{c: s_ for c, s_ in zip(names[1:], shape[1:])})
            return ap

        taken[0] = 0
        qT = part([KD, TOK])
        kT = [part([KD, TOK]) for _ in range(P // DH)]
        v_sb = [part([TT, D]) for _ in range(2)]
        probs = [part([4, S]) for _ in range(2)]
        probsT = [part([2, 4 * P]) for _ in range(2)]
        probsT.append(h_res[:].rearrange("p (k t) d -> p k (t d)", k=2))
        oT_sb = part([KD, TOK])
        k_all = oT_sb
        scaled = [part([4, S]) for _ in range(3)]
        neg_max = part([TT, HEADS])
        row_sum = part([TT, HEADS])
        row_rec = part([TT, HEADS])
        taken[0] = 0
        q8 = part([TT, D], BF16)
        q8T = part([KD, TOK], BF16)
        absmax = part([TT])
        q_scale = part([TT])
        q_back = part([TT])
        diag = part([TT, P])
        back_rows = part([TOK])
        up = [part([TOK]) for _ in range(3)]
        act = part([MH, TOK])
        rounded = [part([HID]) for _ in range(2)]
        q8h = [part([HID], BF16) for _ in range(2)]
        q8hT = [part([MH, P], BF16) for _ in range(2)]
        taken[0] = 0
        w_up_f = part([KD, HID])
        w_down_f = part([MH, D])
        w_sum = part([2])
        w_scale = part([2])
        causal_f = part([P])
        window_f = part([S])
        taken[0] = 0
        xp = part([DT, TOK])
        gate_res = part([DT, TOK])
        xs = part([DT, TOK])
        delta = part([DT, TOK])
        du = part([DT, TOK])
        dA = [part([NC, TOK]) for _ in range(2)]
        hbuf = [part([NC, TOK]) for _ in range(3)]
        b_bc = [part([NC, TOK]) for _ in range(2)]
        c_bc = [part([NC, TOK]) for _ in range(2)]
        last_tap = [t[:, 0, :] for t in hbuf]
        hbuf += [xT[:], side[:].rearrange("p (n t) s -> p n (t s)", n=NC)]
        HB = len(hbuf)
        low_rank, bc_rest = hbuf[4][:, 0, :], hbuf[4][:, 1, :]
        both = xn[:].rearrange("p t d -> p (t d)").bitcast(BF16)
        bc, bc_round = both[:, 0:TOK], both[:, TOK:2 * TOK]
        BC_ROWS = slice(DTR, DTR + 2 * NS)
        taken[0] = 0
        tT = part([KD, TOK])
        t_part = [part([KD, TOK], BF16) for _ in range(3)]
        t_head = [part([2, TOK], BF16) for _ in range(MHD)]
        lg = part([TT * MHD, EXP])
        pr = part([TT * MHD, EXP])
        pick = part([TT * MHD, EXP])
        first = part([TT * MHD, EXP])
        left = part([TT * MHD, EXP])
        best = part([TT * MHD])
        z_sum = part([TT * MHD])
        gates = part([TT, MHD * EXP])
        gatesT = part([TOK])
        gates_rest = left.rearrange("p g e -> p (g e)").rearrange("p (t c) -> p t c", t=TT)
        gates_part = [part([TT, P], BF16) for _ in range(3)]
        gate_blocks = part([4, TOK], BF16)
        hmid = [part([4, TOK]) for _ in range(2)]
        t_rest = hmid[1][:, 0:KD, :]
        gate_bc = [part([TOK]) for _ in range(2)]
        prod = [part([TOK]) for _ in range(2)]
        acc = part([KD, TOK])

        block = ctx.enter_context(nc.Block())

        RES_BANK = (0, 0, 4, 4, 0, 0)

        def of(k, t):
            return slice(t * P, (t + 1) * P)

        def of_half(half):
            return slice(half * EXP // 2, (half + 1) * EXP // 2)

        def attn_shape(n, tt):
            return 1 if n == 0 and tt % 2 == 0 else 2

        def qv_banks(n):
            return (4, 0) if n == 2 else (0, 4)

        def halves(t):
            return t[:].rearrange("p (g h) d -> p g h d", g=PAIR)

        @block.sync
        def _(sp):
            def load(dst, src, name):
                sp.dma_start(dst, src).then_inc(sem[name], 16)

            def cols(name):
                return a[name].rearrange("(k p) n -> p k n", p=P)

            x_v = a["x"].rearrange("(n g) (h p) d -> n p g h d", g=PAIR, p=P)
            ctx_v = a["ctx"].rearrange("(n g) (h p) d -> n p g h d", g=PAIR, p=P)
            side_v = a["side"].rearrange("(n g) (h p) d -> n p g h d", g=PAIR, p=P)
            mask_v = a["mask"].rearrange("(n g) (h p) d -> n p g h d", g=PAIR, p=P)

            def load_ctx(turn):
                for g in range(PAIR):
                    sp.dma_start(halves(ctx_in)[:, g], ctx_v[turn, :, g]).then_inc(sem["ctx_loaded"], 16)

            def load_x(turn):
                for g in range(PAIR):
                    sp.dma_start(halves(x_in)[:, g], x_v[turn, :, g]).then_inc(sem["x_loaded"], 16)

            def load_side(turn):
                for g in range(PAIR):
                    sp.dma_start(halves(side)[:, g], side_v[turn, :, g]).then_inc(sem["side_loaded"], 16)

            def load_mask(turn):
                for g in range(PAIR):
                    sp.dma_start(halves(mask_in)[:, g], mask_v[turn, :, g]).then_inc(sem["mask_loaded"], 16)

            for dst, name in [(ident[:], "c_ident"), (causal_f, "c_causal"), (window_f, "c_window"),
                              (small[:], "small")]:
                load(dst, a[name], "const_loaded")
            for j in range(4):
                for half in range(2):
                    load(w_e1_f[half][32 * j:32 * j + 32], a["W1"][half * EXP // 2:(half + 1) * EXP // 2]
                         .rearrange("e d i -> d e i"), "expert_w_loaded")
            load(w_up_f, cols("w1T"), "ternary_loaded")
            load(w_down_f, cols("w2T"), "ternary_loaded")
            load_ctx(0)
            load_x(0)
            load(w_qkv[:], cols("qkvT"), "first_w_loaded")
            load(w_attn[0, "o"][:], cols("projT"), "first_w_loaded")
            for n in (1, 2):
                for c in "qkvo":
                    load(w_attn[n, c][:], cols(f"x{n}_{c}T"), "attn_w_loaded")
            for i, name in enumerate(BIAS_ROWS):
                r = 32 * (i % 4)
                load(bias_rows[r:r + 1, i // 4, :], a[name], "attn_w_loaded")
            for l in range(2):
                load(w_in[l][:], cols(f"inT{l}"), "rest_w_loaded")
                load(w_x[l][:], cols(f"xT{l}"), "rest_w_loaded")
                load(w_dt[l][:], a[f"dtT{l}"], "rest_w_loaded")
                load(w_out[l][:], cols(f"outT{l}"), "rest_w_loaded")
            load(norm_f[:], a["norm_f"].partition_broadcast(P), "rest_w_loaded")
            load(w_m[:], cols("Wm"), "rest_w_loaded")
            load(emb[:], a["emb"], "rest_w_loaded")
            load(w_e2[:], a["W2"].rearrange("e i o -> i e o"), "rest_w_loaded")
            load(b_e2[:], a["b2_rows"].rearrange("k p m -> p k m"), "rest_w_loaded")
            load(w_mo[:], cols("Wo"), "rest_w_loaded")

            def run_turn(turn, more):
                sp.wait_ge(sem["ctx_in_used"], 1)
                if more:
                    load_ctx(turn + 1)
                sp.wait_ge(sem["x_in_used"], 1)
                if more:
                    load_x(turn + 1)
                sp.wait_ge(sem["y_ready"], 2 * DT)
                load_side(turn)
                sp.wait_ge(sem["mask_used"], 1)
                if more:
                    load_mask(turn + 1)
                sp.wait_ge(sem["x_done"], 1)
                sp.wait_ge(sem["turn_ended"], 4)
                sp.sem_clear(range(in_turn[0], in_turn[0] + len(in_turn)))
                sp.nop().then_inc(sem["turn_opened"], 1)

            sp.wait_ge(sem["expert_last"], 2)
            sp.wait_ge(sem["expert_w_ready"], 1)
            load_mask(0)
            with sp.Fori(0, TURNS - 1) as turn:
                run_turn(turn, True)
            run_turn(TURNS - 1, False)

        N_CONST, N_ATTN, N_REST = 4, 2 * 4 + len(BIAS_ROWS), 2 * 4 + 1 + 2 + 3

        @block.gpsimd
        def _(pool):
            pool.memset(minus_half[:], -0.5).then_inc(sem["half_set"], 1)
            pool.wait_ge(sem["half_set"], 1)
            pool.nop().then_inc(sem["stored"], 1)
            pool.wait_ge(sem["expert_low"], 2)
            pool.wait_ge(sem["expert_copied"], 1)
            for half in range(2):
                pool.tensor_copy(w_e1[1][96:, of_half(half), :], w_e1_f[half][96:]).then_inc(sem["expert_last"], 1)
                pool.wait_ge(sem["expert_last"], half + 1)
            with pool.Fori(0, TURNS) as turn:
                def power(u):
                    for p in range(2):
                        two = slice(2 * p, 2 * p + 2)
                        pool.wait_ge(sem["var_ready"], 2 * u + p + 1)
                        pool.tensor_tensor(rstd[:, two], var_eps[:, two], minus_half[:, two], ALU.pow)\
                            .then_inc(sem["rstd_ready"], 1)

                def zero_values():
                    for i in range(2):
                        pool.memset(v_sb[i].rearrange("p t (h o d) -> p (t h) o d", o=2, d=DH)[:, :, 1 - i], 0.0)\
                            .then_inc(sem["v_zeroed"], 1)

                def mask_keys(n):
                    pool.wait_ge(sem["k_sb"], KD * (n + 1))
                    for i in range(4):
                        j = 4 + i
                        ins = pool.tensor_scalar(kT[j][:, KD - 1, :], k_all[:, KD - 1, :], head_rows[:, j:j + 1], None,
                                                 ALU.mult)
                    ins.then_inc(sem["k_masked_pool"], 1)

                power(0)
                zero_values()
                mask_keys(0)
                power(1)
                mask_keys(1)
                power(2)
                power(3)
                for l in range(2):
                    power(4 + l)
                    for m in range(1, DT):
                        pool.wait_ge(sem["conv5_mid"], DT * l + m + 1)
                        pool.wait_ge(sem["last_tap_ready"], (DT - 1) * l + m)
                        o, tap = (t.rearrange("p (g s) -> p g s", g=PAIR) for t in (xs[:, m, :], last_tap[m - 1]))
                        pool.tensor_tensor(o[:, :, :-2], o[:, :, :-2], tap[:, :, 2:], ALU.add)\
                            .then_inc(sem["last_tap_added"], 1)
                    for s in range(STEPS):
                        c = s // DT
                        if s % DT == 0:
                            pool.wait_ge(sem["c_bc_ready"], l * CHUNKS + c + 1)
                        pool.wait_ge(sem["h_ready"], l * STEPS + s + 1)
                        pool.tensor_tensor(hbuf[s % HB], hbuf[s % HB], c_bc[c % 2], ALU.mult)\
                            .then_inc(sem["hc_ready"], 1)
                power(6)
                zero_values()
                power(7)
                mask_keys(2)
                for g in range(GROUPS):
                    pool.wait_ge(sem["scaled_ready"], g + 1)
                    keep = mask_in[:].bitcast(F32)[:, g // QUADS:g // QUADS + 1, :].to_broadcast([P, 4, S])
                    pool.tensor_tensor(scaled[g % 3], scaled[g % 3], keep, ALU.add)\
                        .then_inc(sem["masked_ready"], 1)
                power(8)
                for v in range(EXP * KD):
                    pool.wait_ge(sem["prod_ready"], v + 1)
                    if v >= KD:
                        pool.wait_ge(sem["acc_added"], v - 1)
                    else:
                        pool.wait_ge(sem["acc_set"], v + 1)
                    pool.tensor_tensor(acc[:, v % KD, :], acc[:, v % KD, :], prod[v % 2], ALU.add)\
                        .then_inc(sem["acc_added"], 1)
                end_turn(pool, turn)

        @block.scalar
        def _(actv):
            out_v = out.rearrange("(n g) (h p) d -> n p g h d", g=PAIR, p=P)
            actv.wait_ge(sem["const_loaded"], 16 * N_CONST)
            for l in range(2):
                actv.activation(decay[l], decay[l], ACT.Exp).then_inc(sem["decay_exp"], 1)
            actv.wait_ge(sem["expert_w_loaded"], 16 * 8)
            for half in range(2):
                actv.activation(w_e1[0][:, of_half(half), :], w_e1_f[half], ACT.Copy).then_inc(sem["expert_high"], 1)
            for half in range(2):
                actv.wait_ge(sem["expert_rest"], half + 1)
                actv.activation(w_e1[1][:, of_half(half), :], w_e1_f[half], ACT.Copy).then_inc(sem["expert_middle"], 1)
            actv.wait_ge(sem["w_scale_ready"], 1)
            for i, w in enumerate((w_up_f, w_down_f)):
                flat = w.rearrange("p a b -> p (a b)")
                actv.activation(flat, flat, ACT.Identity, scale=w_scale[:, i:i + 1], bias=magic[:, 0:1])\
                    .then_inc(sem["w_scaled"], 1)
            actv.wait_ge(sem["expert_low"], 2)
            for half in range(2):
                ins = actv.activation(w_e1[1][32:64, of_half(half), :], w_e1_f[half][32:64], ACT.Copy)
            ins.then_inc(sem["expert_w_ready"], 1)
            with actv.Fori(0, TURNS) as turn:
                order = [0]

                def in_order(ins):
                    ins.then_inc(sem["act_order"], 1)
                    order[0] += 1
                    actv.wait_ge(sem["act_order"], order[0])

                def flip_out(t, dst, scale=None, tiles=1):
                    for k in range(tiles):
                        actv.wait_ge(sem["flip_ps"], KD * t + k + 1)
                        if scale is None:
                            ins = actv.activation(dst[:, k, :], ps[:, 6 + k, :], ACT.Copy)
                        else:
                            ins = actv.activation(dst[:, k, :], ps[:, 6 + k, :], ACT.Copy, scale=scale[:, k:k + 1])
                        ins.then_inc(sem["flip_sb"], 1)

                def keys_values(n):
                    for k in range(KD):
                        actv.wait_ge(sem["k_ps"], KD * n + k + 1)
                        if n == 0:
                            ins = actv.activation(k_all[:, k, :], ps[:, 2 + k, :], ACT.Copy)
                        else:
                            ins = actv.activation(k_all[:, k, :], ps[:, 2 + k, :], ACT.Identity,
                                                  bias=b_qk[n][:, 1, k:k + 1])
                        ins.then_inc(sem["k_sb"], 1)
                    for k in range(2):
                        actv.wait_ge(sem["v_ps"], 2 * n + k + 1)
                        for i in range(2):
                            actv.activation(
                                v_sb[i][:, 2 * k:2 * k + 2, :].rearrange("p t (h o d) -> p (t h) o d", o=2, d=DH)[:, :, i],
                                ps[:, qv_banks(n)[1] + k, :].rearrange("p (h o d) -> p h o d", o=2, d=DH)[:, :, i],
                                ACT.Copy).then_inc(sem["v_sb"], 1)

                def queries(n):
                    for k in range(KD):
                        actv.wait_ge(sem["q_ps"], KD * n + k + 1)
                        if n == 0:
                            ins = actv.activation(qT[:, k, :], ps[:, qv_banks(n)[0] + k, :], ACT.Copy, scale=DH ** -0.5)
                        else:
                            ins = actv.activation(qT[:, k, :], ps[:, qv_banks(n)[0] + k, :], ACT.Identity,
                                                  scale=DH ** -0.5, bias=b_qk[n][:, 0, k:k + 1])
                        ins.then_inc(sem["q_sb"], 1)

                def attention(n):
                    def evacuate(g):
                        actv.wait_ge(sem["probsT_ps"], GROUPS * n + g + 1)
                        if g >= 3:
                            actv.wait_ge(sem["pv_done"], PAIRS * n + (g - 3) // 2 + 1)
                        actv.activation(probsT[g % 3], ps[:, 4:6, :], ACT.Copy).then_inc(sem["probsT_sb"], 1)

                    for g in range(GROUPS):
                        tt, c = g // QUADS, g % QUADS
                        w = attn_shape(n, tt) * P
                        actv.wait_ge(sem["max_ready"], GROUPS * n + g + 1)
                        if g >= 2:
                            actv.wait_ge(sem["probsT_ps"], GROUPS * n + g - 1)
                        for i in range(4):
                            if n == 2:
                                src = scaled[g % 3][:, i, :]
                            else:
                                src = ps[:, 2 * (g % 2) + i // 2, 256 * (i % 2):256 * (i % 2) + w]
                            h = 4 * c + i
                            ins = actv.activation(probs[g % 2][:, i, 0:w], src, ACT.Exp,
                                                  bias=neg_max[:, tt, h:h + 1],
                                                  accum_out=row_sum[:, tt, h:h + 1])
                        ins.then_inc(sem["probs_ready"], 1)
                        if n == 2 and g >= 1:
                            evacuate(g - 1)
                    if n == 2:
                        evacuate(GROUPS - 1)
                    actv.wait_ge(sem["pv_done"], PAIRS * (n + 1))
                    actv.activation(oT_sb, ps[:, 6:8, :], ACT.Copy).then_inc(sem["oT_ready"], 1)

                def ffn():
                    actv.wait_ge(sem["q8T_ps"], 1)
                    actv.activation(q8T.rearrange("p k t -> p (k t)"), ps[:, 6, :].bitcast(BF16),
                                    ACT.Copy).then_inc(sem["q8T_sb"], 1)
                    actv.wait_ge(sem["back_ps"], 1)
                    actv.activation(back_rows, ps[:, 7, :], ACT.Copy, scale=unquant[:, 0:1])\
                        .then_inc(sem["back_sb"], 1)
                    for m in range(MH + 1):
                        if m < MH:
                            actv.wait_ge(sem["up_sb"], m + 1)
                            actv.activation(act[:, m, :], up[m % 3], ACT.Identity, scale=conv3_w[:, m, 1:2],
                                            bias=conv3_b[:, m:m + 1]).then_inc(sem["conv_mid"], 1)
                        if m >= 1:
                            actv.wait_ge(sem["conv3_done"], m)
                            actv.activation(act[:, m - 1, :], act[:, m - 1, :], ACT.Silu)\
                                .then_inc(sem["act_ready"], 1)
                    for t in range(TT + 1):
                        if t < TT:
                            actv.wait_ge(sem["scale2_ready"], t + 1)
                            actv.activation(rounded[t % 2], ps[:, 2 * (t % 2):2 * (t % 2) + 2, :].rearrange("p a b -> p (a b)"),
                                            ACT.Identity, scale=q_scale[:, t:t + 1], bias=magic[:, 0:1])\
                                .then_inc(sem["rounded_ready"], 1)
                        if t >= 1:
                            actv.wait_ge(sem["q8hT_ps"], t)
                            actv.activation(q8hT[(t - 1) % 2].rearrange("p m t -> p (m t)"),
                                            ps[:, 4 + (t - 1) % 2, :].bitcast(BF16), ACT.Copy)\
                                .then_inc(sem["q8hT_sb"], 1)

                def load_exp_table():
                    actv.activation(scratch[:], ones[:, 0:1], ACT.Exp)

                def mamba(l):
                    flip_out(5 + l, xT, norm_w[l])
                    def conv_silu(m):
                        actv.wait_ge(sem["conv5_done"], DT * l + m + 1)
                        actv.activation(xs[:, m, :], xs[:, m, :], ACT.Silu).then_inc(sem["xs_ready"], 1)

                    for m in range(DT):
                        actv.wait_ge(sem["in_ps"], 2 * DT * l + m + 1)
                        actv.activation(xp[:, m, :], ps[:, m, :], ACT.Identity, bias=b_in[l][:, m:m + 1])\
                            .then_inc(sem["in_sb"], 1)
                        actv.wait_ge(sem["in_sb"], DT * l + m + 1)
                        actv.activation(xs[:, m, :], xp[:, m, :], ACT.Identity, scale=conv5_w[l][:, m, 2:3],
                                        bias=conv5_b[l][:, m:m + 1]).then_inc(sem["conv5_mid"], 1)
                        if m >= 1:
                            actv.activation(last_tap[m - 1], xp[:, m, :], ACT.Copy, scale=conv5_w[l][:, m, 4:5])\
                                .then_inc(sem["last_tap_ready"], 1)
                    for m in range(EARLY_Z):
                        actv.wait_ge(sem["in_ps"], 2 * DT * l + DT + m + 1)
                        actv.activation(gate_res[:, m, :], ps[:, m, :], ACT.Silu,
                                        bias=b_in[l][:, DT + m:DT + m + 1]).then_inc(sem["gate_ready"], 1)
                        conv_silu(m)
                    for m in range(EARLY_Z, DT):
                        conv_silu(m)
                    load_exp_table()
                    actv.wait_ge(sem["xdbl_ps"], l + 1)
                    actv.activation(low_rank[0:DTR, :], ps[0:DTR, 4, :], ACT.Copy).then_inc(sem["low_rank_sb"], 1)
                    actv.activation(bc_rest[BC_ROWS, :], ps[BC_ROWS, 4, :], ACT.Copy).then_inc(sem["bc_sb"], 1)
                    actv.activation(bc[0:2 * NS, :], ps[BC_ROWS, 4, :], ACT.Copy).then_inc(sem["bc_sb"], 1)
                    for m in range(DT):
                        actv.wait_ge(sem["dt_ps"], DT * l + m + 1)
                        actv.activation(delta[:, m, :], ps[:, m, :], ACT.Identity, bias=b_dt[l][:, m:m + 1])\
                            .then_inc(sem["z_sb"], 1)
                    for m in range(DT):
                        actv.wait_ge(sem["abs_ready"], DT * l + m + 1)
                        ins = actv.activation(xp[:, m, :], xp[:, m, :], ACT.Exp, scale=-1.0)
                    in_order(ins)
                    for m in range(DT):
                        actv.activation(xp[:, m, :], xp[:, m, :], ACT.Ln, bias=ones[:, 0:1]).then_inc(sem["ln_ready"], 1)
                    for s in range(STEPS):
                        c, m = s // DT, s % DT
                        if s < DT:
                            actv.wait_ge(sem["delta_ready"], l * DT + m + 1)
                        if s >= 2:
                            actv.wait_ge(sem["h_ready"], l * STEPS + s - 1)
                        for i in range(NC):
                            n = c * NC + i
                            ins = actv.activation(dA[s % 2][:, i, :].rearrange("p (g t) -> p g t", g=PAIR)[:, :, 1:],
                                                  delta[:, m, :].rearrange("p (g t) -> p g t", g=PAIR)[:, :, 1:],
                                                  ACT.Exp, scale=decay[l][:, m, n:n + 1])
                        ins.then_inc(sem["dA_ready"], 1)
                        if m == 1 and c + 1 < CHUNKS:
                            b_out(l, c + 1)
                        if m == 3 and c + 1 < CHUNKS:
                            c_out(l, c + 1)
                    actv.wait_ge(sem["late_z_sb"], (DT - EARLY_Z) * (l + 1))
                    for m in range(EARLY_Z, DT):
                        actv.activation(gate_res[:, m, :], gate_res[:, m, :], ACT.Silu).then_inc(sem["gate_ready"], 1)

                def b_out(l, c):
                    actv.wait_ge(sem["bc_ps"], l * CHUNKS + c + 1)
                    if c >= 2:
                        actv.wait_ge(sem["injected"], l * STEPS + DT * (c - 1))
                    actv.activation(b_bc[c % 2], ps[:, 4:6, :], ACT.Copy).then_inc(sem["b_bc_ready"], 1)

                def c_out(l, c):
                    if c >= 2:
                        actv.wait_ge(sem["hc_ready"], l * STEPS + DT * (c - 1))
                    actv.activation(c_bc[c % 2], ps[:, 6:8, :], ACT.Copy).then_inc(sem["c_bc_ready"], 1)

                def moe():
                    flip_out(9, xT)
                    for k in range(KD):
                        actv.wait_ge(sem["t_ps"], k + 1)
                        actv.activation(tT[:, k, :], ps[:, k, :], ACT.Identity, bias=b_m[:, k:k + 1])\
                            .then_inc(sem["t_sb"], 1)
                    actv.wait_ge(sem["t_sb"], KD)
                    actv.activation(t_part[0], tT, ACT.Copy).then_inc(sem["t_high"], 1)
                    actv.wait_ge(sem["t_rest_ready"], 1)
                    actv.activation(t_part[1], t_rest, ACT.Copy).then_inc(sem["t_high"], 1)
                    actv.wait_ge(sem["logits_ready"], 1)
                    actv.activation(pr, lg, ACT.Exp).then_inc(sem["router_exp"], 1)
                    for h in range(MHD):
                        actv.wait_ge(sem["t_head_ps"], h + 1)
                        actv.activation(t_head[h], ps[:, 2 * (h % 2):2 * (h % 2) + 2, :], ACT.Copy)\
                            .then_inc(sem["t_head_sb"], 1)

                    def gelu(w):
                        v, e = w // 2, w // 4
                        actv.wait_ge(sem["up_e_ps"], w + 1)
                        if w % 2 == 0 and v >= 2:
                            actv.wait_ge(sem["down_e_done"], v - 1)
                        actv.activation(hmid[v % 2][:, 2 * (w % 2):2 * (w % 2) + 2, :],
                                        ps[:, 2 * (w % 2):2 * (w % 2) + 2, :], ACT.Gelu,
                                        bias=b_e1[:, e:e + 1]).then_inc(sem["hmid_ready"], 1)

                    for w in range(UP_AHEAD):
                        gelu(w)
                    actv.wait_ge(sem["gatesT_ps"], 1)
                    actv.activation(gatesT, ps[:, 6, :], ACT.Copy).then_inc(sem["gatesT_sb"], 1)
                    for k in range(KD):
                        actv.wait_ge(sem["b2_ps"], k + 1)
                        actv.activation(acc[:, k, :], ps[:, 4 + k, :], ACT.Copy).then_inc(sem["acc_set"], 1)
                    for b in range(4):
                        actv.wait_ge(sem["block_ps"], b + 1)
                        actv.activation(gate_blocks[0:96, b, :], ps[0:96, 6 + b % 2, :], ACT.Copy)\
                            .then_inc(sem["block_sb"], 1)
                    for w in range(UP_AHEAD, EXP * KD * 2):
                        gelu(w)

                flip_out(0, ctxT, tiles=KD)
                flip_out(1, xT)
                queries(0)
                keys_values(0)
                attention(0)
                keys_values(1)
                flip_out(3, xT)
                queries(1)
                attention(1)
                ffn()
                mamba(0)
                mamba(1)
                keys_values(2)
                flip_out(7, xT)
                queries(2)
                attention(2)
                moe()
                actv.wait_ge(sem["x_done"], 1)
                for g in range(PAIR):
                    actv.dma_start(out_v[turn, :, g], halves(x)[:, g]).then_inc(sem["stored"], 16)
                end_turn(actv, turn)
            actv.wait_ge(sem["stored"], TURNS * PAIR * 16 + 1)

        @block.vector
        def _(dve):
            setup = [0]

            def in_setup_order(ins):
                ins.then_inc(sem["dve_setup"], 1)
                setup[0] += 1
                dve.wait_ge(sem["dve_setup"], setup[0])

            dve.memset(magic[:], ROUND)
            in_setup_order(dve.memset(ones[:], 1.0))
            dve.wait_ge(sem["const_loaded"], 16 * N_CONST)
            for i in range(3):
                rows = slice(2 * NS * i, 2 * NS * (i + 1))
                dve.tensor_copy(same_of_three[rows, :], ident[rows, rows])
            for exact, src in [(ident_bf, ident[:]), (causal_bf, causal_f), (window_bf, window_f)]:
                dve.tensor_copy(exact[:], src)
            for i in range(3):
                rows = slice(32 * i, 32 * i + 32)
                dve.tensor_copy(gate_sel[rows].rearrange("p u (j r) -> p (u j) r", j=4),
                                ident[rows, rows].unsqueeze(2).to_broadcast([32, 32, MD]))
            for half in range(2):
                dve.wait_ge(sem["expert_high"], half + 1)
                dve.tensor_tensor(w_e1_f[half], w_e1_f[half], w_e1[0][:, of_half(half), :], ALU.subtract)\
                    .then_inc(sem["expert_rest"], 1)
            dve.wait_ge(sem["ternary_loaded"], 16 * 2)
            flat_w = [w_up_f.rearrange("p a b -> p (a b)"), w_down_f.rearrange("p a b -> p (a b)")]
            flat_q = [w_up[:].rearrange("p a b -> p (a b)"), w_down[:].rearrange("p a b -> p (a b)")]
            for i in range(2):
                ins = dve.tensor_reduce(w_sum[:, i:i + 1], flat_w[i], AX.X, ALU.add, apply_absolute_value=True)
            ins.then_inc(sem["w_sum_ready"], 1)
            dve.wait_ge(sem["w_sum_ps"], 1)
            in_setup_order(dve.tensor_scalar(unquant[:], ps[:, 0, 0:2], 1.0 / (D * HID), 1e-5, ALU.mult, ALU.max))
            dve.reciprocal(w_scale, unquant[:]).then_inc(sem["w_scale_ready"], 1)
            dve.wait_ge(sem["expert_middle"], 2)
            dve.wait_ge(sem["expert_rest"], 2)
            dve.tensor_copy(w_e1[0][3 * 32:, :, :], w_e1[1][3 * 32:, :, :]).then_inc(sem["expert_copied"], 1)
            for half in range(2):
                dve.tensor_tensor(w_e1_f[half], w_e1_f[half], w_e1[1][:, of_half(half), :], ALU.subtract)\
                    .then_inc(sem["expert_low"], 1)
            dve.wait_ge(sem["expert_copied"], 1)
            dve.wait_ge(sem["w_scaled"], 2)
            for i in range(2):
                dve.tensor_scalar(flat_w[i], flat_w[i], ROUND, 1.0, ALU.subtract, ALU.min)\
                    .then_inc(sem["dve_setup"], 1)
                setup[0] += 1
            dve.wait_ge(sem["dve_setup"], setup[0])
            for i in range(2):
                in_setup_order(dve.tensor_scalar(flat_q[i], flat_w[i], -1.0, None, ALU.max))
            dve.nop().then_inc(sem["ternary_ready"], 1)
            dve.wait_ge(sem["decay_exp"], 2)
            for l in range(2):
                in_setup_order(dve.tensor_scalar(decay[l], decay[l], -1.0, None, ALU.mult))
            for n in (1, 2):
                ins = dve.tensor_scalar(b_qk[n][:, 0, :], b_qk[n][:, 0, :], DH ** -0.5, None, ALU.mult)
            in_setup_order(ins)
            dve.nop().then_inc(sem["setup_done"], 1)

            with dve.Fori(0, TURNS) as turn:
                order = [0]

                def mark(ins):
                    ins.then_inc(sem["dve_order"], 1)
                    order[0] += 1

                def in_order(ins=None):
                    if ins is not None:
                        mark(ins)
                    dve.wait_ge(sem["dve_order"], order[0])

                def norm(u, src, rms=False, dst=None, add=None, weight=None):
                    dst = xn if dst is None else dst
                    for p in range(2):
                        two = slice(2 * p, 2 * p + 2)
                        if add is not None:
                            r, other = add
                            dve.wait_ge(sem["res_ps"], 2 * r + p + 1)
                            in_order(dve.tensor_tensor(src[:, two, :], other[:, two, :],
                                                       ps[:, RES_BANK[r] + p, :].rearrange("p (t d) -> p t d", t=2), ALU.add))
                        for t in (2 * p, 2 * p + 1):
                            ins = dve.bn_stats(stats[:, t, :], src[:, t, :])
                        in_order(ins)
                        for t in (2 * p, 2 * p + 1):
                            ins = dve.bn_aggr(mean_var[:, t, :], stats[:, t, :])
                        in_order(ins)
                        mean, var = mean_var[:, two, 0], mean_var[:, two, 1]
                        if rms:
                            in_order(dve.tensor_tensor(sq[:, two], mean, mean, ALU.mult))
                            ins = dve.scalar_tensor_tensor(out=var_eps[:, two], in0=var, scalar=EPS, in1=sq[:, two],
                                                           op0=ALU.add, op1=ALU.add)
                        else:
                            ins = dve.tensor_scalar(var_eps[:, two], var, EPS, None, ALU.add)
                        ins.then_inc(sem["var_ready"], 1)
                    for t in range(TT):
                        if t % 2 == 0:
                            dve.wait_ge(sem["rstd_ready"], 2 * u + t // 2 + 1)
                        if weight is not None:
                            ins = dve.scalar_tensor_tensor(out=dst[:, t, :], in0=src[:, t, :], scalar=rstd[:, t:t + 1],
                                                           in1=weight, op0=ALU.mult, op1=ALU.mult)
                        elif rms:
                            ins = dve.tensor_scalar(dst[:, t, :], src[:, t, :], rstd[:, t:t + 1], None, ALU.mult)
                        else:
                            ins = dve.tensor_scalar(dst[:, t, :], src[:, t, :], mean_var[:, t, 0:1],
                                                    rstd[:, t:t + 1], ALU.subtract, ALU.mult)
                        ins.then_inc(sem["xn_ready"], 1)

                def flip_out(t, scale=None):
                    dve.wait_ge(sem["flip_ps"], KD * t + 2)
                    if scale is None:
                        ins = dve.tensor_copy(xT[:, 1, :], ps[:, 7, :])
                    else:
                        ins = dve.tensor_scalar(xT[:, 1, :], ps[:, 7, :], scale[:, 1:2], None, ALU.mult)
                    ins.then_inc(sem["flip_sb"], 1)

                def residual(r, src, dst):
                    for p in range(2):
                        dve.wait_ge(sem["res_ps"], 2 * r + p + 1)
                        mark(dve.tensor_tensor(dst[:, 2 * p:2 * p + 2, :], src[:, 2 * p:2 * p + 2, :],
                                               ps[:, p, :].rearrange("p (t d) -> p t d", t=2), ALU.add))
                    in_order()

                def attention(n):
                    for g in range(POOL_QUAD):
                        dve.wait_ge(sem["k_sb"], KD * n + g // 2 + 1)
                        for i in range(4):
                            j, m = 4 * (g % 2) + i, g // 2
                            ins = dve.tensor_scalar(kT[j][:, m, :], k_all[:, m, :], head_rows[:, j:j + 1], None, ALU.mult)
                        ins.then_inc(sem["k_masked"], 1)

                    def maxima(g):
                        tt, c = g // QUADS, g % QUADS
                        w = attn_shape(n, tt) * P
                        if n == 2:
                            dve.wait_ge(sem["masked_ready"], g + 1)
                            src = scaled[g % 3]
                        else:
                            dve.wait_ge(sem["scores_ps"], GROUPS * n + g + 1)
                            src = ps[:, 2 * (g % 2):2 * (g % 2) + 2, :].rearrange("p a (b c) -> p (a b) c", b=2)[:, :, 0:w]
                        dve.tensor_reduce(neg_max[:, tt, 4 * c:4 * c + 4], src, AX.X, ALU.max, negate=True)\
                            .then_inc(sem["max_ready"], 1)

                    def scale(g):
                        dve.wait_ge(sem["scores_ps"], GROUPS * n + g + 1)
                        if g >= 3:
                            dve.wait_ge(sem["probs_ready"], GROUPS * n + g - 2)
                        rows = side[:, g // QUADS:g // QUADS + 1, :].to_broadcast([P, 4, S])
                        src = ps[:, 2 * (g % 2):2 * (g % 2) + 2, :].rearrange("p a (b c) -> p (a b) c", b=2)
                        dve.tensor_tensor(scaled[g % 3], src, rows, ALU.mult).then_inc(sem["scaled_ready"], 1)

                    def evacuate(g):
                        dve.wait_ge(sem["probsT_ps"], GROUPS * n + g + 1)
                        if g >= 3:
                            dve.wait_ge(sem["pv_done"], PAIRS * n + (g - 3) // 2 + 1)
                        w = attn_shape(n, g // QUADS)
                        dve.tensor_copy(probsT[g % 3][:, 0:w, :], ps[:, 4:4 + w, :]).then_inc(sem["probsT_sb"], 1)

                    def inverse(tt):
                        dve.wait_ge(sem["probs_ready"], GROUPS * n + QUADS * (tt + 1))
                        in_order(dve.reciprocal(row_rec[:, tt, :], row_sum[:, tt, :]))
                        dve.tensor_copy(xn[:, tt, :].rearrange("p (h d) -> p h d", d=DH),
                                        row_rec[:, tt, :].unsqueeze(2).to_broadcast([P, HEADS, DH]))\
                            .then_inc(sem["inverse_ready"], 1)

                    for g in range(GROUPS + 1):
                        if n == 2:
                            if g < GROUPS:
                                scale(g)
                            if g >= 1:
                                maxima(g - 1)
                        else:
                            if g < GROUPS:
                                maxima(g)
                            if g >= 1:
                                evacuate(g - 1)
                        if g % QUADS == 2 and g > QUADS:
                            inverse(g // QUADS - 1)
                    inverse(TT - 1)
                    for k in range(KD):
                        dve.wait_ge(sem["oT_ready"], n + 1)
                        dve.wait_ge(sem["flip_ps"], KD * [2, 4, 8][n] + k + 1)
                        dve.tensor_tensor(xT[:, k, :], oT_sb[:, k, :], ps[:, 2 + k, :], ALU.mult).then_inc(sem["flip_sb"], 1)

                def ffn():
                    norm(2, x, add=(1, x))
                    dve.wait_ge(sem["xn_ready"], 4 * 3)
                    in_order(dve.tensor_reduce(absmax, xn[:], AX.X, ALU.max, apply_absolute_value=True))
                    in_order(dve.tensor_scalar(absmax, absmax, 1e-5, None, ALU.max))
                    in_order(dve.reciprocal(q_scale, absmax))
                    in_order(dve.tensor_scalar(q_scale, q_scale, 127.0, None, ALU.mult))
                    for t in range(TT):
                        mark(dve.tensor_scalar(xn[:, t, :], xn[:, t, :], q_scale[:, t:t + 1], ROUND, ALU.mult, ALU.add))
                    in_order()
                    in_order(dve.tensor_scalar(xn[:], xn[:], ROUND, -128.0, ALU.subtract, ALU.max))
                    dve.tensor_scalar(q8, xn[:], 127.0, None, ALU.min).then_inc(sem["q8_ready"], 1)
                    in_order(dve.reciprocal(q_back, q_scale))
                    for t in range(TT):
                        dve.tensor_scalar(diag[:, t, :], ident[:], q_back[:, t:t + 1], None, ALU.mult)\
                            .then_inc(sem["diag_ready"], 1)
                    dve.wait_ge(sem["back_sb"], 1)

                    def rows(t):
                        return t.rearrange("p (g s) -> p g s", g=PAIR)

                    def take_up(m):
                        dve.wait_ge(sem["up_ps"], m + 1)
                        if m >= 3:
                            dve.wait_ge(sem["conv3_done"], m - 2)
                        dve.tensor_tensor(up[m % 3], ps[:, m % 4, :], back_rows, ALU.mult).then_inc(sem["up_sb"], 1)

                    take_up(0)
                    take_up(1)
                    for m in range(MH):
                        dve.wait_ge(sem["conv_mid"], m + 1)
                        dve.wait_ge(sem["up_sb"], m + 1)
                        o, u = rows(act[:, m, :]), rows(up[m % 3])
                        mark(dve.scalar_tensor_tensor(out=o[:, :, 1:], in0=u[:, :, :-1], scalar=conv3_w[:, m, 0:1],
                                                      in1=o[:, :, 1:], op0=ALU.mult, op1=ALU.add))
                        if m + 2 < MH:
                            take_up(m + 2)
                        in_order()
                        dve.scalar_tensor_tensor(out=o[:, :, :-1], in0=u[:, :, 1:], scalar=conv3_w[:, m, 2:3],
                                                 in1=o[:, :, :-1], op0=ALU.mult, op1=ALU.add)\
                            .then_inc(sem["conv3_done"], 1)

                    for t in range(TT + 2):
                        if t < TT:
                            dve.wait_ge(sem["actT_ps"], t + 1)
                            src = ps[:, 2 * (t % 2):2 * (t % 2) + 2, :].rearrange("p a b -> p (a b)")
                            one = slice(t, t + 1)
                            in_order(dve.tensor_reduce(absmax[:, one], src, AX.X, ALU.max, apply_absolute_value=True))
                            in_order(dve.tensor_scalar(absmax[:, one], absmax[:, one], 1e-5, None, ALU.max))
                            in_order(dve.reciprocal(q_scale[:, one], absmax[:, one]))
                            dve.tensor_scalar(q_scale[:, one], q_scale[:, one], 127.0, None, ALU.mult)\
                                .then_inc(sem["scale2_ready"], 1)
                            dve.wait_ge(sem["scale2_ready"], t + 1)
                            in_order(dve.reciprocal(q_back[:, one], q_scale[:, one]))
                            in_order(dve.tensor_scalar(q_back[:, one], q_back[:, one], unquant[:, 1:2], None, ALU.mult))
                        if 1 <= t <= TT:
                            j = t - 1
                            dve.wait_ge(sem["rounded_ready"], t)
                            if j >= 2:
                                dve.wait_ge(sem["q8hT_ps"], j - 1)
                            in_order(dve.tensor_scalar(rounded[j % 2], rounded[j % 2], ROUND, -128.0, ALU.subtract, ALU.max))
                            dve.tensor_scalar(q8h[j % 2], rounded[j % 2], 127.0, None, ALU.min)\
                                .then_inc(sem["q8h_ready"], 1)
                        if t >= 2:
                            j = t - 2
                            dve.wait_ge(sem["down_ps"], j + 1)
                            in_order(dve.scalar_tensor_tensor(out=x[:, j, :], in0=ps[:, 6 + j % 2, 0:D],
                                                              scalar=q_back[:, j:j + 1], in1=x[:, j, :],
                                                              op0=ALU.mult, op1=ALU.add))

                def mamba(l):
                    norm(4 + l, h_res, rms=True, add=None if l == 0 else (2, h_res))
                    flip_out(5 + l, norm_w[l])

                    def rows(t):
                        return t.rearrange("p (g s) -> p g s", g=PAIR)

                    if l == 0:
                        for i in range(2):
                            dve.memset(dA[i].rearrange("p n (g t) -> p (n g) t", g=PAIR)[:, :, 0:1], 0.0)\
                                .then_inc(sem["dA_heads"], 1)
                    for m in range(DT):
                        if m == 0:
                            dve.wait_ge(sem["conv5_mid"], DT * l + 1)
                        else:
                            dve.wait_ge(sem["last_tap_added"], (DT - 1) * l + m)
                        o, u = rows(xs[:, m, :]), rows(xp[:, m, :])
                        shifts = [(0, -2), (1, -1), (3, 1), (4, 2)][:4 if m == 0 else 3]
                        for k, shift in shifts:
                            if shift < 0:
                                dst, src = o[:, :, -shift:], u[:, :, :shift]
                            else:
                                dst, src = o[:, :, :-shift], u[:, :, shift:]
                            ins = dve.scalar_tensor_tensor(out=dst, in0=src, scalar=conv5_w[l][:, m, k:k + 1], in1=dst,
                                                           op0=ALU.mult, op1=ALU.add)
                            if (k, shift) != shifts[-1]:
                                in_order(ins)
                        ins.then_inc(sem["conv5_done"], 1)
                    dve.wait_ge(sem["bc_sb"], 2 * l + 1)
                    for i in range(1, 3):
                        in_order(dve.tensor_copy(bc_round[BC_ROWS, :], bc_rest[BC_ROWS, :]))
                        if i == 1:
                            in_order(dve.tensor_tensor(bc_rest[BC_ROWS, :], bc_rest[BC_ROWS, :], bc_round[BC_ROWS, :],
                                                       ALU.subtract))
                            dve.tensor_copy(bc[2 * NS:4 * NS, :], bc_rest[BC_ROWS, :]).then_inc(sem["bc_split"], 1)
                        else:
                            dve.tensor_tensor(bc[BC_ROWS, :], bc_rest[BC_ROWS, :], bc_round[BC_ROWS, :], ALU.subtract)\
                                .then_inc(sem["bc_split"], 1)
                    for m in range(DT):
                        dve.wait_ge(sem["z_sb"], DT * l + m + 1)
                        dve.scalar_tensor_tensor(out=xp[:, m, :], in0=delta[:, m, :], scalar=-1.0, in1=delta[:, m, :],
                                                 op0=ALU.mult, op1=ALU.max).then_inc(sem["abs_ready"], 1)
                    dve.wait_ge(sem["bc_ps"], l * CHUNKS + 1)
                    dve.tensor_copy(b_bc[0], ps[:, 4:6, :]).then_inc(sem["b_bc_ready"], 1)
                    dve.tensor_copy(c_bc[0], ps[:, 6:8, :]).then_inc(sem["c_bc_ready"], 1)
                    for m in range(EARLY_Z, DT):
                        dve.wait_ge(sem["in_ps"], 2 * DT * l + DT + m + 1)
                        dve.tensor_scalar(gate_res[:, m, :], ps[:, m, :], b_in[l][:, DT + m:DT + m + 1], None, ALU.add)\
                            .then_inc(sem["late_z_sb"], 1)

                    def inject(s):
                        c, m = s // DT, s % DT
                        if m == 0:
                            dve.wait_ge(sem["b_bc_ready"], l * CHUNKS + c + 1)
                        if s >= HB:
                            dve.wait_ge(sem["y_added"], l * STEPS + s - HB + 1)
                        dve.tensor_tensor(hbuf[s % HB], du[:, m:m + 1, :].to_broadcast([P, NC, TOK]), b_bc[c % 2], ALU.mult)\
                            .then_inc(sem["injected"], 1)

                    def prepare(s):
                        if s < DT:
                            dve.wait_ge(sem["ln_ready"], DT * l + s + 1)
                            dve.wait_ge(sem["xs_ready"], DT * l + s + 1)
                            dve.scalar_tensor_tensor(out=delta[:, s, :], in0=delta[:, s, :], scalar=0.0, in1=xp[:, s, :],
                                                     op0=ALU.max, op1=ALU.add).then_inc(sem["delta_ready"], 1)
                            dve.wait_ge(sem["delta_ready"], DT * l + s + 1)
                            in_order(dve.tensor_tensor(du[:, s, :], delta[:, s, :], xs[:, s, :], ALU.mult))
                        inject(s)

                    prepare(0)
                    for s in range(STEPS):
                        if s + 1 < STEPS:
                            prepare(s + 1)
                        dve.wait_ge(sem["dA_ready"], l * STEPS + s + 1)
                        dve.wait_ge(sem["injected"], l * STEPS + s + 1)
                        if s == 0 and l == 0:
                            dve.wait_ge(sem["dA_heads"], 2)
                        flat = hbuf[s % HB].rearrange("p n t -> p (n t)")
                        dve.tensor_tensor_scan(flat, dA[s % 2].rearrange("p n t -> p (n t)"), flat, 0.0,
                                               ALU.mult, ALU.add).then_inc(sem["h_ready"], 1)
                    for m in range(DT):
                        dve.wait_ge(sem["y_added"], l * STEPS + STEPS - DT + m + 1)
                        in_order(dve.scalar_tensor_tensor(out=xp[:, m, :], in0=xs[:, m, :], scalar=skip[l][:, m:m + 1],
                                                          in1=ps[:, m, :], op0=ALU.mult, op1=ALU.add))
                        dve.wait_ge(sem["gate_ready"], DT * l + m + 1)
                        dve.tensor_tensor(xp[:, m, :], xp[:, m, :], gate_res[:, m, :], ALU.mult)\
                            .then_inc(sem["y_ready"], 1)

                def moe():
                    norm(8, x, add=(4, x))
                    flip_out(9)
                    groups = TT * MHD

                    def over(t):
                        return t.unsqueeze(2).to_broadcast([P, groups, EXP])

                    dve.wait_ge(sem["t_high"], 1)
                    dve.tensor_tensor(t_rest, tT, t_part[0], ALU.subtract).then_inc(sem["t_rest_ready"], 1)
                    dve.wait_ge(sem["t_high"], 2)
                    dve.tensor_tensor(t_part[2], t_rest, t_part[1], ALU.subtract).then_inc(sem["t_split"], 1)
                    dve.wait_ge(sem["logits_ps"], 1)
                    logit = ps[:, 7, :].rearrange("p (g e) -> p g e", e=EXP)
                    in_order(dve.tensor_reduce(best, logit, AX.X, ALU.max))
                    dve.tensor_tensor(lg, logit, over(best), ALU.subtract).then_inc(sem["logits_ready"], 1)
                    dve.wait_ge(sem["router_exp"], 1)
                    in_order(dve.tensor_reduce(z_sum, pr, AX.X, ALU.add))
                    in_order(dve.reciprocal(z_sum, z_sum))
                    in_order(dve.tensor_tensor(pr, pr, over(z_sum), ALU.mult))
                    ranks = rank.unsqueeze(1).to_broadcast([P, groups, EXP])

                    def choose(values, chosen):
                        in_order(dve.tensor_reduce(best, values, AX.X, ALU.max))
                        in_order(dve.tensor_tensor(pick, values, over(best), ALU.is_equal))
                        in_order(dve.tensor_tensor(pick, pick, ranks, ALU.mult))
                        in_order(dve.tensor_reduce(best, pick, AX.X, ALU.max))
                        in_order(dve.tensor_tensor(chosen, pick, over(best), ALU.is_equal))

                    choose(pr, first)
                    flat = "p g e -> p (g e)"
                    in_order(dve.scalar_tensor_tensor(out=left.rearrange(flat), in0=first.rearrange(flat), scalar=-2.0,
                                                      in1=pr.rearrange(flat), op0=ALU.mult, op1=ALU.add))
                    choose(left, lg)
                    in_order(dve.tensor_tensor(first, first, lg, ALU.add))
                    split = "p (t h) e -> p t h e"
                    dve.tensor_tensor(gates.rearrange("p t (e h) -> p t h e", e=EXP), pr.rearrange(split, t=TT),
                                      first.rearrange(split, t=TT), ALU.mult).then_inc(sem["gates_ready"], 1)
                    dve.wait_ge(sem["gates_ready"], 1)
                    in_order(dve.tensor_copy(gates_part[0], gates))
                    in_order(dve.tensor_tensor(gates_rest, gates, gates_part[0], ALU.subtract))
                    in_order(dve.tensor_copy(gates_part[1], gates_rest))
                    dve.tensor_tensor(gates_part[2], gates_rest, gates_part[1], ALU.subtract)\
                        .then_inc(sem["gates_split"], 1)
                    for v in range(EXP * KD):
                        dve.wait_ge(sem["gate_ps"], v + 1)
                        dve.tensor_copy(gate_bc[v % 2], ps[:, 6 + v % 2, :]).then_inc(sem["gate_sb"], 1)
                        dve.wait_ge(sem["down_e_done"], v + 1)
                        dve.wait_ge(sem["gate_sb"], v + 1)
                        if v >= 2:
                            dve.wait_ge(sem["acc_added"], v - 1)
                        dve.tensor_tensor(prod[v % 2], ps[:, 4 + v % 2, :], gate_bc[v % 2], ALU.mult)\
                            .then_inc(sem["prod_ready"], 1)
                    residual(5, x, x)

                dve.wait_ge(sem["x_loaded"], PAIR * 16 * (turn + 1))
                norm(0, x_in)
                flip_out(1)
                attention(0)
                dve.wait_ge(sem["stored"], PAIR * 16 * turn + 1)
                norm(1, x, add=(0, x_in))
                dve.nop().then_inc(sem["x_in_used"], 1)
                flip_out(3)
                attention(1)
                dve.wait_ge(sem["mask_loaded"], PAIR * 16 * (turn + 1))
                in_order(dve.tensor_scalar(mask_in[:].bitcast(F32), mask_in[:], 0, -1e30, ALU.is_equal, ALU.mult))
                ffn()
                norm(3, x, dst=h_res)
                dve.wait_ge(sem["xn_ready"], 4 * 4)
                mamba(0)
                mamba(1)
                norm(6, h_res, rms=True, add=(3, h_res), weight=norm_f[:])
                dve.wait_ge(sem["xn_ready"], 4 * 7)
                in_order(dve.tensor_tensor(x[:], x[:], xn[:], ALU.add))
                norm(7, x)
                flip_out(7)
                dve.wait_ge(sem["side_loaded"], PAIR * 16 * (turn + 1))
                attention(2)
                dve.nop().then_inc(sem["mask_used"], 1)
                moe()
                dve.nop().then_inc(sem["x_done"], 1)
                end_turn(dve, turn)

        @block.tensor
        def _(pe):
            pe.wait_ge(sem["const_loaded"], 16 * N_CONST)
            pe.wait_ge(sem["dve_setup"], 1)
            pe.wait_ge(sem["w_sum_ready"], 1)
            pe.matmul(ps[:, 0, 0:2], ones[:], w_sum, start=True, stop=True).then_inc(sem["w_sum_ps"], 1)
            pe.wait_ge(sem["setup_done"], 1)
            pe.wait_ge(sem["ternary_ready"], 1)
            pe.wait_ge(sem["first_w_loaded"], 16 * 2)

            with pe.Fori(0, TURNS) as turn:
                def flip(t, src, name, first_count, bank=6):
                    for tt in range(TT):
                        pe.wait_ge(sem[name], first_count + tt)
                        for k in range(KD):
                            ins = pe.transpose(ps[:, bank + k, of(0, tt)], src[:, tt, k * P:(k + 1) * P], ident[:])
                            if tt == TT - 1:
                                ins.then_inc(sem["flip_ps"], 1)

                def add_bias(bank, i):
                    b0 = 32 * (i % 4)
                    pe.matmul(bank.rearrange("p (t d) -> p t d", t=2), ones[b0:b0 + 1, :],
                              bias_rows[b0:b0 + 1, i // 4:i // 4 + 1, :].to_broadcast([1, 2, D]), start=True, stop=False)

                def project_tokens(r, src, w, bias, tiles, ready):
                    def piece(tt, k):
                        return pe.matmul(ps[:, RES_BANK[r] + tt // 2, (tt % 2) * D:(tt % 2 + 1) * D], src[:, k, of(0, tt)], w[:, k, :],
                                         start=(k == 0 and tt % 2 == 0 and bias is None),
                                         stop=(k == tiles - 1 and tt % 2 == 1))

                    if bias is not None:
                        for p in range(2):
                            add_bias(ps[:, RES_BANK[r] + p, :], bias)
                    for k in range(tiles - 1):
                        pe.wait_ge(sem[ready[0]], ready[1] + k)
                        for tt in range(TT):
                            piece(tt, k)
                    pe.wait_ge(sem[ready[0]], ready[1] + tiles - 1)
                    for tt in range(TT):
                        ins = piece(tt, tiles - 1)
                        if tt % 2:
                            ins.then_inc(sem["res_ps"], 1)

                def weights(n, c):
                    i = "qkv".index(c)
                    return w_qkv[:, :, i * D:(i + 1) * D] if n == 0 else w_attn[n, c][:]

                def queries(n):
                    pe.wait_ge(sem["flip_sb"], 2 * [1, 3, 7][n] + 2)
                    for m in range(KD):
                        for k in range(KD):
                            ins = pe.matmul(ps[:, qv_banks(n)[0] + m, :], weights(n, "q")[:, k, m * P:(m + 1) * P], xT[:, k, :],
                                            start=(k == 0), stop=(k == KD - 1))
                        ins.then_inc(sem["q_ps"], 1)

                def keys_values(n):
                    kv = xT if n == 0 else ctxT
                    if n == 1:
                        pe.wait_ge(sem["attn_w_loaded"], 16 * N_ATTN)
                    for m in range(KD):
                        for k in range(KD):
                            ins = pe.matmul(ps[:, 2 + m, :], weights(n, "k")[:, k, m * P:(m + 1) * P], kv[:, k, :],
                                            start=(k == 0), stop=(k == KD - 1))
                        ins.then_inc(sem["k_ps"], 1)
                    for tt in range(TT):
                        dst = ps[:, qv_banks(n)[1] + tt // 2, (tt % 2) * D:(tt % 2 + 1) * D]
                        if n > 0 and tt % 2 == 0:
                            add_bias(ps[:, qv_banks(n)[1] + tt // 2, :], 2 * (n - 1))
                        for k in range(KD):
                            ins = pe.matmul(dst, kv[:, k, of(0, tt)], weights(n, "v")[:, k, :],
                                            start=(k == 0 and n == 0 and tt % 2 == 0),
                                            stop=(k == KD - 1 and tt % 2 == 1))
                        if tt % 2:
                            ins.then_inc(sem["v_ps"], 1)

                def attention(n):
                    def scores(g):
                        tt, c = g // QUADS, g % QUADS
                        b = tt // 2
                        w_ = attn_shape(n, tt) * P
                        if g >= 2:
                            if n == 2:
                                pe.wait_ge(sem["scaled_ready"], g - 1)
                            else:
                                pe.wait_ge(sem["probs_ready"], GROUPS * n + g - 1)
                        if g < POOL_QUAD:
                            pe.wait_ge(sem["k_masked"], POOL_QUAD * n + g + 1)
                        elif g == POOL_QUAD:
                            pe.wait_ge(sem["k_masked_pool"], n + 1)
                        masked = n == 0 or (n == 1 and tt % 2 == 0)
                        for i in range(4):
                            h = 4 * c + i
                            m, j = h // 8, h % 8
                            dst = ps[:, 2 * (g % 2) + i // 2, 256 * (i % 2):256 * (i % 2) + w_]
                            ins = pe.matmul(dst, qT[:, m, of(0, tt)], kT[j][:, m, b * S:b * S + w_],
                                            start=True, stop=not masked)
                            if masked and n == 0:
                                ins = pe.matmul(dst[:, w_ - P:w_], ident_bf[:], causal_bf[:], start=False, stop=True)
                            elif masked:
                                ins = pe.matmul(dst, ident_bf[:], window_bf[:], start=False, stop=True)
                        ins.then_inc(sem["scores_ps"], 1)

                    def turn_probs(g):
                        pe.wait_ge(sem["probs_ready"], GROUPS * n + g + 1)
                        if g >= 1:
                            pe.wait_ge(sem["probsT_sb"], GROUPS * n + g)
                        for kt in range(attn_shape(n, g // QUADS)):
                            for i in range(4):
                                ins = pe.transpose(ps[:, 4 + kt, i * P:(i + 1) * P],
                                                   probs[g % 2][:, i, kt * P:(kt + 1) * P], ident[:])
                        ins.then_inc(sem["probsT_ps"], 1)

                    def values(p):
                        tt, c = 2 * p // QUADS, p % (QUADS // 2)
                        pe.wait_ge(sem["probsT_sb"], GROUPS * n + 2 * p + 2)
                        kts = attn_shape(n, tt)
                        for kt in range(kts):
                            for odd in range(2):
                                for j in range(4):
                                    g, i = 2 * p + j // 2, 2 * (j % 2) + odd
                                    lo = P * c + 32 * j
                                    ins = pe.matmul(ps[32 * j:32 * j + 32, 6 + c, of(0, tt)],
                                                    v_sb[odd][:, 2 * (tt // 2) + kt, lo:lo + 32],
                                                    probsT[g % 3][:, kt, i * P:(i + 1) * P],
                                                    start=(kt == 0 and odd == 0), stop=(kt == kts - 1 and odd == 1))
                        ins.then_inc(sem["pv_done"], 1)

                    pe.wait_ge(sem["q_sb"], KD * (n + 1))
                    pe.wait_ge(sem["k_sb"], KD * (n + 1))
                    pe.wait_ge(sem["v_sb"], 4 * (n + 1))
                    pe.wait_ge(sem["v_zeroed"], 4 if n == 2 else 2)
                    ahead = 3 if n == 2 else 1
                    for g in range(ahead):
                        scores(g)
                    for g in range(GROUPS):
                        if g + ahead < GROUPS:
                            scores(g + ahead)
                        turn_probs(g)
                        if g >= 2 and g % 2 == 0:
                            values(g // 2 - 1)
                    values(PAIRS - 1)
                    flip([2, 4, 8][n], xn, "inverse_ready", TT * n + 1, bank=2)
                    project_tokens([0, 1, 4][n], xT, w_attn[n, "o"], None if n == 0 else 2 * n - 1, KD,
                                   ("flip_sb", KD * [2, 4, 8][n] + 1))

                def ffn():
                    pe.wait_ge(sem["q8_ready"], 1)
                    flat = ps[:, 6, :].bitcast(BF16)
                    for k in range(KD):
                        for tt in range(TT):
                            ins = pe.transpose(flat[:, k * TOK + tt * P:k * TOK + (tt + 1) * P],
                                               q8[:, tt, k * P:(k + 1) * P], ident_bf[:])
                    ins.then_inc(sem["q8T_ps"], 1)
                    pe.wait_ge(sem["diag_ready"], TT)
                    for tt in range(TT):
                        ins = pe.matmul(ps[:, 7, of(0, tt)], ones[:], diag[:, tt, :], start=True, stop=True)
                    ins.then_inc(sem["back_ps"], 1)
                    pe.wait_ge(sem["q8T_sb"], 1)
                    for m in range(MH):
                        if m >= 4:
                            pe.wait_ge(sem["up_sb"], m - 3)
                        for k in range(KD):
                            ins = pe.matmul(ps[:, m % 4, :], w_up[:, k, m * P:(m + 1) * P], q8T[:, k, :],
                                            start=(k == 0), stop=(k == KD - 1))
                        ins.then_inc(sem["up_ps"], 1)
                    pe.wait_ge(sem["up_sb"], MH)
                    for m in range(MH):
                        pe.wait_ge(sem["act_ready"], m + 1)
                        for tt in range(2):
                            ins = pe.transpose(ps[:, 2 * tt + m // 4, (m % 4) * P:(m % 4 + 1) * P], act[:, m, of(0, tt)],
                                               ident[:])
                            if m == MH - 1:
                                ins.then_inc(sem["actT_ps"], 1)

                    def turn_act(tt):
                        pe.wait_ge(sem["rounded_ready"], tt - 1)
                        for m in range(MH):
                            bank = 2 * (tt % 2) + m // 4
                            ins = pe.transpose(ps[:, bank, (m % 4) * P:(m % 4 + 1) * P], act[:, m, of(0, tt)], ident[:])
                        ins.then_inc(sem["actT_ps"], 1)

                    for tt in range(TT):
                        pe.wait_ge(sem["q8h_ready"], tt + 1)
                        if tt >= 2:
                            pe.wait_ge(sem["q8hT_sb"], tt - 1)
                        flat = ps[:, 4 + tt % 2, :].bitcast(BF16)
                        for m in range(MH):
                            ins = pe.transpose(flat[:, m * P:(m + 1) * P], q8h[tt % 2][:, m * P:(m + 1) * P], ident_bf[:])
                        ins.then_inc(sem["q8hT_ps"], 1)
                        if tt + 2 < TT:
                            turn_act(tt + 2)
                        pe.wait_ge(sem["q8hT_sb"], tt + 1)
                        for m in range(MH):
                            ins = pe.matmul(ps[:, 6 + tt % 2, 0:D], q8hT[tt % 2][:, m, :], w_down[:, m, :],
                                            start=(m == 0), stop=(m == MH - 1))
                        ins.then_inc(sem["down_ps"], 1)

                def mamba(l):
                    if l == 0:
                        pe.wait_ge(sem["rest_w_loaded"], 16 * N_REST)
                    flip(5 + l, xn, "xn_ready", 4 * (4 + l) + 1)
                    pe.wait_ge(sem["flip_sb"], 2 * (5 + l) + 2)

                    def project_in(m):
                        for k in range(KD):
                            ins = pe.matmul(ps[:, m % 4, :], w_in[l][:, k, m * P:(m + 1) * P], xT[:, k, :],
                                            start=(k == 0), stop=(k == KD - 1))
                        ins.then_inc(sem["in_ps"], 1)

                    for m in range(DT):
                        project_in(m)
                    for m in range(EARLY_Z):
                        pe.wait_ge(sem["in_sb"], DT * l + m + 1)
                        project_in(DT + m)
                    for m in range(DT):
                        pe.wait_ge(sem["xs_ready"], DT * l + m + 1)
                        ins = pe.matmul(ps[0:DTR + 2 * NS, 4, :], w_x[l][:, m, :], xs[:, m, :],
                                        start=(m == 0), stop=(m == DT - 1))
                    ins.then_inc(sem["xdbl_ps"], 1)
                    pe.wait_ge(sem["low_rank_sb"], l + 1)
                    for m in range(DT):
                        pe.matmul(ps[:, m, :], w_dt[l][:, m * P:(m + 1) * P], low_rank[0:DTR, :], start=True, stop=True)\
                            .then_inc(sem["dt_ps"], 1)
                    pe.wait_ge(sem["bc_split"], 2 * (l + 1))
                    pe.wait_ge(sem["bc_sb"], 2 * (l + 1))

                    def spread(c):
                        if c >= 1:
                            pe.wait_ge(sem["c_bc_ready"], l * CHUNKS + c)
                        for i in range(NC):
                            for which in range(2):
                                r = which * NS + c * NC + i
                                ins = pe.matmul(ps[:, 4 + 2 * which + i, :],
                                                same_of_three[0:BC3, r:r + 1].to_broadcast([BC3, P]),
                                                bc[0:BC3, :], start=True, stop=True)
                        ins.then_inc(sem["bc_ps"], 1)

                    spread(0)
                    pe.wait_ge(sem["z_sb"], DT * (l + 1))
                    for m in range(EARLY_Z, DT):
                        project_in(DT + m)
                    pe.wait_ge(sem["late_z_sb"], (DT - EARLY_Z) * (l + 1))
                    for s in range(STEPS):
                        c, m = s // DT, s % DT
                        if s == 0:
                            spread(1)
                        if m == 2 and c + 2 < CHUNKS:
                            spread(c + 2)
                        pe.wait_ge(sem["hc_ready"], l * STEPS + s + 1)
                        for i in range(NC):
                            ins = pe.matmul(ps[:, m, :], ident[:], hbuf[s % HB][:, i, :], start=(c == 0 and i == 0),
                                            stop=(c == CHUNKS - 1 and i == NC - 1))
                        ins.then_inc(sem["y_added"], 1)
                    project_tokens(2 + l, xp, w_out[l], 4 + l, DT, ("y_ready", DT * l + 1))

                def moe():
                    pe.wait_ge(sem["expert_w_ready"], 1)
                    pe.wait_ge(sem["expert_last"], 2)
                    pe.wait_ge(sem["expert_copied"], 1)
                    flip(9, xn, "xn_ready", 4 * 8 + 1)
                    pe.wait_ge(sem["flip_sb"], 20)
                    for m in range(KD):
                        for k in range(KD):
                            ins = pe.matmul(ps[:, m, :], w_m[:, k, m * P:(m + 1) * P], xT[:, k, :],
                                            start=(k == 0), stop=(k == KD - 1))
                        ins.then_inc(sem["t_ps"], 1)
                    pe.wait_ge(sem["t_sb"], KD)
                    for tt in range(TT):
                        for k in range(KD):
                            at = (tt * KD + k) * 4 * EXP
                            ins = pe.matmul(ps[:, 7, at:at + 4 * EXP], tT[:, k, of(0, tt)], emb[:], start=True, stop=True)
                    ins.then_inc(sem["logits_ps"], 1)
                    pe.wait_ge(sem["t_high"], 2)
                    pe.wait_ge(sem["t_split"], 1)
                    for h in range(MHD):
                        if h >= 2:
                            pe.wait_ge(sem["t_head_sb"], h - 1)
                        cols = slice(32 * (h % 4), 32 * (h % 4) + 32)
                        for i, order in enumerate(T_PARTS):
                            for j, which in enumerate(order):
                                ins = pe.matmul(ps[32 * j:32 * j + 32, 2 * (h % 2) + i, :], ident_bf[:, cols],
                                                t_part[which][:, h // 4, :], start=True, stop=True)
                        ins.then_inc(sem["t_head_ps"], 1)

                    def up_e(w):
                        e, k, half = w // 4, w // 2 % 2, w % 2
                        if w >= 2:
                            pe.wait_ge(sem["hmid_ready"], w - 1)
                        if w < 2:
                            pe.wait_ge(sem["t_head_sb"], MHD - 1 + w)
                        for i in range(2):
                            for which in range(2):
                                ins = pe.matmul(ps[:, 2 * (w % 2) + i, :], w_e1[which][:, e, :],
                                                t_head[4 * k + 2 * half + i][:, which, :],
                                                start=(which == 0), stop=(which == 1))
                        ins.then_inc(sem["up_e_ps"], 1)

                    def spread_gate(v):
                        if v >= 2:
                            pe.wait_ge(sem["gate_sb"], v - 1)
                        ins = pe.matmul(ps[:, 6 + v % 2, :], gate_sel[0:96, v % 8, :], gate_blocks[0:96, v // 8, :],
                                        start=True, stop=True)
                        ins.then_inc(sem["gate_ps"], 1)

                    def gated_bias(k):
                        pe.matmul(ps[:, 4 + k, :], b_e2[:, k, :], gatesT, start=True, stop=True).then_inc(sem["b2_ps"], 1)

                    for w in range(UP_AHEAD):
                        up_e(w)
                    pe.wait_ge(sem["gates_ready"], 1)
                    for tt in range(TT):
                        ins = pe.transpose(ps[:, 6, of(0, tt)], gates[:, tt, :], ident[:])
                    ins.then_inc(sem["gatesT_ps"], 1)
                    pe.wait_ge(sem["gatesT_sb"], 1)
                    gated_bias(0)
                    gated_bias(1)
                    pe.wait_ge(sem["gates_split"], 1)
                    for b in range(4):
                        if b >= 2:
                            pe.wait_ge(sem["block_sb"], b - 1)
                        for tt in range(TT):
                            for i in range(3):
                                ins = pe.matmul(ps[32 * i:32 * i + 32, 6 + b % 2, of(0, tt)],
                                                gates_part[i][:, tt, 32 * b:32 * b + 32], ident_bf[:],
                                                start=(tt == 0), stop=(tt == TT - 1))
                        ins.then_inc(sem["block_ps"], 1)
                    pe.wait_ge(sem["block_sb"], 3)
                    spread_gate(0)
                    for v in range(EXP * KD):
                        if v == 0:
                            pe.wait_ge(sem["block_sb"], 4)
                        if v + 1 < EXP * KD:
                            spread_gate(v + 1)
                        pe.wait_ge(sem["hmid_ready"], 2 * v + 2)
                        if v >= 2:
                            pe.wait_ge(sem["prod_ready"], v - 1)
                        else:
                            pe.wait_ge(sem["acc_set"], v + 1)
                        for j in range(4):
                            ins = pe.matmul(ps[32 * j:32 * j + 32, 4 + v % 2, :], w_e2[:, v // KD, :],
                                            hmid[v % 2][:, j, :], start=True, stop=True)
                        ins.then_inc(sem["down_e_done"], 1)
                        for w in (2 * v + UP_AHEAD, 2 * v + UP_AHEAD + 1):
                            if w < EXP * KD * 2:
                                up_e(w)
                    project_tokens(5, acc, w_mo, 6, KD, ("acc_added", EXP * KD - 1))

                pe.wait_ge(sem["ctx_loaded"], PAIR * 16 * (turn + 1))
                for tt in range(TT):
                    for k in range(KD):
                        ins = pe.transpose(ps[:, 6 + k, of(0, tt)], ctx_in[:, tt, k * P:(k + 1) * P], ident[:])
                        if tt == TT - 1:
                            ins.then_inc(sem["flip_ps"], 1)
                pe.wait_ge(sem["flip_sb"], 2)
                pe.nop().then_inc(sem["ctx_in_used"], 1)
                flip(1, xn, "xn_ready", 1)
                queries(0)
                keys_values(0)
                attention(0)
                keys_values(1)
                flip(3, xn, "xn_ready", 5)
                queries(1)
                attention(1)
                ffn()
                mamba(0)
                mamba(1)
                keys_values(2)
                flip(7, xn, "xn_ready", 29)
                queries(2)
                attention(2)
                moe()
                end_turn(pe, turn)


def layouts(inp):
    import numpy as np

    def arr(name):
        return np.asarray(inp[name])

    def T(w):
        return np.ascontiguousarray(w.T)

    a = {"x": arr("x"), "ctx": arr("ctx_1024"), "side": arr("fside_BxSxS2_0"),
         "mask": arr("mask_Bx1xSxS2_if1").reshape(B, S, S)}
    a["qkvT"], a["projT"] = T(arr("L0_attn_w_qkv")), T(arr("L0_attn_w_proj"))
    small = {}

    def by_partition(v):
        v = v.reshape(-1, P, *v.shape[1:])
        return np.moveaxis(v, 1, 0).reshape(P, -1)

    for n, pre in ((1, "L0_xattn_"), (2, "L1_xattn_")):
        for c in "qkvo":
            a[f"x{n}_{c}T"] = T(arr(f"{pre}W{c}"))
        small[f"b_qk{n}"] = np.concatenate([by_partition(arr(pre + "bq")), by_partition(arr(pre + "bk"))], 1)
        for c in "vo":
            a[f"{pre}b{c}"] = arr(f"{pre}b{c}").reshape(1, D)
    a["w1T"], a["w2T"] = T(arr("L0_ffn_w1")), T(arr("L0_ffn_w2"))
    small["conv3_w"] = by_partition(arr("L0_ffn_conv_w").reshape(HID, 3))
    small["conv3_b"] = by_partition(arr("L0_ffn_conv_b"))
    for l in range(2):
        m = "L1_attn_"
        a[f"inT{l}"], a[f"xT{l}"] = T(arr(m + "in_proj_w")[l]), T(arr(m + "x_proj_w")[l])
        a[f"dtT{l}"], a[f"outT{l}"] = T(arr(m + "dt_proj_w")[l]), T(arr(m + "out_proj_w")[l])
        a[f"out_b{l}"] = arr(m + "out_proj_b")[l].reshape(1, D)
        small[f"conv5_w{l}"] = by_partition(arr(m + "conv_w")[l].reshape(DI, TAPS))
        for name, source in [("b_in", "in_proj_b"), ("conv5_b", "conv_b"), ("b_dt", "dt_proj_b"), ("decay", "A_log"),
                             ("skip", "D"), ("norm_w", "norm_w")]:
            small[f"{name}{l}"] = by_partition(arr(m + source)[l])
    a["norm_f"] = arr("L1_attn_norm_f_w")
    f = "L1_ffn_"
    a["Wm"], a["Wo"], a["W1"], a["W2"] = (arr(f + c) for c in ("Wm", "Wo", "W1", "W2"))
    a["L1_ffn_bo"] = arr(f + "bo").reshape(1, D)
    small["b_m"], small["b_e1"] = by_partition(arr(f + "bm")), arr(f + "b1").T
    emb = np.zeros((P, 4 * EXP), np.float32)
    b2 = np.zeros((KD, MHD * EXP, P), np.float32)
    for j in range(4):
        emb[32 * j:32 * j + 32, EXP * j:EXP * (j + 1)] = arr(f + "expert_emb")
        for k in range(KD):
            h = 4 * k + j
            b2[k, h::MHD, MD * j:MD * (j + 1)] = arr(f + "b2")
    a["emb"], a["b2_rows"] = emb, b2
    i, j = np.arange(P)[:, None], np.arange(S)[None, :]
    a["c_ident"] = np.eye(P, dtype=np.float32)
    a["c_causal"] = np.where(j[:, :P] > i, -1e30, 0.0).astype(np.float32)
    a["c_window"] = np.where(j // 4 > i, -1e30, 0.0).astype(np.float32)
    small["head_rows"] = (np.arange(P)[:, None] // DH == np.arange(P // DH)).astype(np.float32)
    small["rank"] = np.tile(np.arange(EXP, 0, -1, dtype=np.float32), (P, 1))
    a["small"] = np.concatenate([small[name] for name, _ in SMALL], 1)
    return {k: np.ascontiguousarray(v) for k, v in a.items()}


def kernel(**inputs):
    import concourse.bacc as bacc
    from concourse.bass_utils import run_bass_kernel_spmd as run

    arrays = layouts(inputs)
    nc = bacc.Bacc("TRN2", target_bir_lowering=False, num_devices=1)
    aps = {k: nc.dram_tensor(f"in_{k}", v.shape, mybir.dt.from_np(v.dtype), kind="ExternalInput").ap()
           for k, v in arrays.items()}
    out = nc.dram_tensor("out_0", (B, S, D), F32, kind="ExternalOutput").ap()
    program(nc, aps, out)
    r = run(nc, [{f"in_{k}": v for k, v in arrays.items()}], core_ids=[0])
    return r.results[0]["out_0"]
```
